# Optimizing a Trainium2 kernel written in Bass

```python
import numpy as np
import jax
import jax.numpy as jnp

def _softmax(x, axis=-1):
    return jax.nn.softmax(x, axis=axis)

def _gelu(x):
    return jax.nn.gelu(x, approximate=True)

def _silu(x):
    return jax.nn.silu(x)

def _sigmoid(x):
    return jax.nn.sigmoid(x)

def _layernorm(x, axis=-1, eps=1e-05):
    m = jnp.mean(x, axis=axis, keepdims=True)
    v = jnp.var(x, axis=axis, keepdims=True)
    return (x - m) / jnp.sqrt(v + eps)

def _scatter_add(tgt, idx, src, axis=0):
    return tgt.at[idx].add(src)

def _segment_sum(src, seg, n):
    return jax.ops.segment_sum(src, seg, n)
kernel_name = 'mk_gnn_ffn_d1_gnn_r8_205588'

def setup_inputs(seed: int=0):
    np.random.seed(seed)
    _w = jnp.asarray

    def _rec_inputs():
        import jax
        import jax.numpy as jnp
        _gk = jax.random.key(seed)
        x = -0.0003713 + 1 * jax.random.normal(jax.random.fold_in(_gk, 1), (6250, 256), jnp.float32)
        _s = jax.random.randint(jax.random.fold_in(_gk, 2), (50000,), 0, 6250, jnp.int32)
        _d = jax.random.randint(jax.random.fold_in(_gk, 3), (50000,), 0, 6250, jnp.int32)
        _loop = jnp.arange(6250, dtype=jnp.int32)
        src = jnp.concatenate([_s, _d, _loop])
        dst = jnp.concatenate([_d, _s, _loop])
        _o = jnp.argsort(dst, stable=True)
        src = src[_o]
        dst = dst[_o]
        edge_type_16 = jax.random.randint(jax.random.fold_in(_gk, 12), (106250,), 0, 16, jnp.int32)
        edge_weight1 = jax.random.uniform(jax.random.fold_in(_gk, 13), (106250, 1), jnp.float32, 0.0, 1)
        return (x, src, dst, edge_type_16, edge_weight1)
    x, src, dst, edge_type_16, edge_weight1 = _rec_inputs()

    def _L0_gnn_setup():
        import jax, jax.numpy as jnp
        import numpy as np
        N_NODES = 6250
        N_EDGES = 100000
        NUM_RELS = 16
        FEAT = 256
        OUT = 256
        key = jax.random.key(seed)
        ks = jax.random.split(key, 7)
        h = jax.random.normal(ks[0], (N_NODES, FEAT), dtype=jnp.float32)
        norm = jax.random.uniform(ks[1], (N_EDGES, 1), dtype=jnp.float32)
        weight = jax.random.normal(ks[2], (NUM_RELS, FEAT, OUT), dtype=jnp.float32) * 0.05
        gate_weight = jax.random.normal(ks[3], (NUM_RELS, FEAT, 1), dtype=jnp.float32) * 0.05
        src = jax.random.randint(ks[4], (N_EDGES,), 0, N_NODES)
        dst = jax.random.randint(ks[5], (N_EDGES,), 0, N_NODES)
        rel_type = jax.random.randint(ks[6], (N_EDGES,), 0, NUM_RELS)
        return {'h': h, 'norm': norm, 'weight': weight, 'gate_weight': gate_weight, 'src': src, 'dst': dst, 'rel_type': rel_type}
    _L0_gnn_all = _L0_gnn_setup()
    _L0_gnn_in = {k: v for k, v in _L0_gnn_all.items() if k in ('weight', 'gate_weight')}
    del _L0_gnn_all

    def _L0_ffn_setup():
        import jax, jax.numpy as jnp
        import numpy as np
        NUM_EXPERTS = 8
        TOP_K = 2
        B, S, D = (8, 1024, 256)

        def _moe(tokens, router_w, w1, b1, w2, b2):
            N = tokens.shape[0]
            E = router_w.shape[0]
            logits = tokens.astype(jnp.float32) @ router_w.astype(jnp.float32).T
            probs = jax.nn.softmax(logits, axis=-1)
            rw, re = jax.lax.top_k(probs, TOP_K)
            if TOP_K > 1:
                rw = rw / jnp.maximum(rw.sum(-1, keepdims=True), 1e-12)
            rw = rw.astype(tokens.dtype)
            combine = jnp.zeros((N, E), tokens.dtype).at[jnp.arange(N)[:, None], re].set(rw)
            out = tokens
            for e in range(E):
                h = jax.nn.gelu(tokens @ w1[e] + b1[e], approximate=False)
                y = h @ w2[e] + b2[e]
                out = out + combine[:, e:e + 1] * y
            return out
        key = jax.random.key(seed)
        ks = jax.random.split(key, 4)
        scale = 1.0 / np.sqrt(D).astype(np.float32)
        return {'input_embeddings': jax.random.normal(ks[0], (B, S, D), jnp.float32), 'router_w': jax.random.normal(ks[1], (NUM_EXPERTS, D), jnp.float32) * scale, 'w1': jax.random.normal(ks[2], (NUM_EXPERTS, D, D), jnp.float32) * scale, 'b1': jnp.zeros((NUM_EXPERTS, D), jnp.float32), 'w2': jax.random.normal(ks[3], (NUM_EXPERTS, D, D), jnp.float32) * scale, 'b2': jnp.zeros((NUM_EXPERTS, D), jnp.float32)}
    _L0_ffn_all = _L0_ffn_setup()
    _L0_ffn_in = {k: v for k, v in _L0_ffn_all.items() if k in ('router_w', 'w1', 'b1', 'w2', 'b2')}
    del _L0_ffn_all
    return {'x': x, 'src': src, 'dst': dst, 'edge_type_16': edge_type_16, 'edge_weight1': edge_weight1, 'L0_gnn_weight': _L0_gnn_in['weight'], 'L0_gnn_gate_weight': _L0_gnn_in['gate_weight'], 'L0_ffn_router_w': _L0_ffn_in['router_w'], 'L0_ffn_w1': _L0_ffn_in['w1'], 'L0_ffn_b1': _L0_ffn_in['b1'], 'L0_ffn_w2': _L0_ffn_in['w2'], 'L0_ffn_b2': _L0_ffn_in['b2']}

def reference(x, src, dst, edge_type_16, edge_weight1, L0_gnn_weight, L0_gnn_gate_weight, L0_ffn_router_w, L0_ffn_w1, L0_ffn_b1, L0_ffn_w2, L0_ffn_b2):
    import jax
    import jax.numpy as jnp

    def _L0_gnn_ref(h, norm, weight, gate_weight, src, dst, rel_type):
        import jax, jax.numpy as jnp
        import numpy as np
        N_NODES = 6250
        N_EDGES = 100000
        NUM_RELS = 16
        FEAT = 256
        OUT = 256
        n_nodes = h.shape[0]
        all_msg = jnp.einsum('nf,rfo->rno', h, weight)
        msg = all_msg[rel_type, src] * norm
        all_gate = jnp.einsum('nf,rf->rn', h, gate_weight[..., 0])
        gate = jax.nn.sigmoid(all_gate[rel_type, src])[:, None]
        msg = msg * gate
        agg = jax.ops.segment_sum(msg, dst, num_segments=n_nodes)
        return jax.nn.relu(agg)

    def _L0_ffn_ref(input_embeddings, router_w, w1, b1, w2, b2):
        import jax, jax.numpy as jnp
        import numpy as np
        NUM_EXPERTS = 8
        TOP_K = 2
        B, S, D = (8, 1024, 256)

        def _moe(tokens, router_w, w1, b1, w2, b2):
            N = tokens.shape[0]
            E = router_w.shape[0]
            logits = tokens.astype(jnp.float32) @ router_w.astype(jnp.float32).T
            probs = jax.nn.softmax(logits, axis=-1)
            rw, re = jax.lax.top_k(probs, TOP_K)
            if TOP_K > 1:
                rw = rw / jnp.maximum(rw.sum(-1, keepdims=True), 1e-12)
            rw = rw.astype(tokens.dtype)
            combine = jnp.zeros((N, E), tokens.dtype).at[jnp.arange(N)[:, None], re].set(rw)
            out = tokens
            for e in range(E):
                h = jax.nn.gelu(tokens @ w1[e] + b1[e], approximate=False)
                y = h @ w2[e] + b2[e]
                out = out + combine[:, e:e + 1] * y
            return out
        b, s, d = input_embeddings.shape
        tokens = input_embeddings.reshape(b * s, d)
        return _moe(tokens, router_w, w1, b1, w2, b2).reshape(b, s, d)
    x = x + _L0_gnn_ref(_layernorm(x, axis=-1), edge_weight1, L0_gnn_weight, L0_gnn_gate_weight, src, dst, edge_type_16)
    x = x + _L0_ffn_ref(_layernorm(x, axis=-1)[None], L0_ffn_router_w, L0_ffn_w1, L0_ffn_b1, L0_ffn_w2, L0_ffn_b2)[0]
    return x

_drawn_inputs = setup_inputs


def setup_inputs(seed=0):
    import zlib

    import numpy as np

    out = dict(_drawn_inputs(seed))
    spreads = {'L0_ffn_b1': (0.0, 0.355), 'L0_ffn_b2': (0.0, 0.1)}
    factors = {}
    for name, (base, spread) in spreads.items():
        noise = np.random.default_rng([zlib.crc32(name.encode()), seed]).standard_normal(out[name].shape)
        drawn = base * np.exp(spread * noise) if base else spread * noise
        out[name] = jnp.asarray(drawn.astype(out[name].dtype))
    for name, factor in factors.items():
        out[name] = (out[name] * factor).astype(out[name].dtype)
    return out
```

```python
import concourse.bass as bass
from concourse import mybir
from contextlib import ExitStack

FP32 = mybir.dt.float32
I32 = mybir.dt.int32
ALU = mybir.AluOpType
ACT = mybir.ActivationFunctionType
AX = mybir.AxisListType

N, E, R, F = 6250, 106250, 16, 256
P = 128
KH = F // P
EXP = 8
TILES = -(-N // P)
LAST_ROWS = N - (TILES - 1) * P
BATCH = 2 * P
BATCHES = -(-N // BATCH)
NPAD = BATCHES * BATCH
GROUP = 4 * P
GPI = 8
GROUPS = -(-E // GROUP)
ROUNDS = GROUPS // GPI
FULL = E // GROUP
REST = E - FULL * GROUP
WIN = 128
AGGW = NPAD + WIN
THIRD = (8, 16)
SLOTS = 4
EPS = 1e-5
RSQRT_MAGIC = float(0x5F3759DF)
assert GROUPS == ROUNDS * GPI and P < FULL < 2 * P


class Chain:

    def __init__(self, engine, sem, base=0):
        self.engine, self.sem, self.base, self.n = engine, sem, base, 0

    def __call__(self, instruction):
        instruction.then_inc(self.sem, 1)
        self.n += 1
        self.engine.wait_ge(self.sem, self.base + self.n)


def build(nc, x, src, dst, etype, eweight, gw, ggate, router, w1, b1, w2, b2, out):
    assert GPI * 4 * F == R * F * 2
    table = nc.dram_tensor("message_table", (N * R, F), FP32, kind="Internal").ap()
    group_dram = nc.dram_tensor("group_numbers", (2 * P, 2), FP32, kind="Internal").ap()
    ctx = ExitStack()
    with ctx:
        def sb(name, shape, dt=FP32):
            return ctx.enter_context(nc.sbuf_tensor(name, shape, dt))

        def sem(name):
            return ctx.enter_context(nc.semaphore(name))

        res = sb("res", [P, 2 * BATCHES, F])
        agg = sb("agg", [P, KH * AGGW])
        aggv = agg[:, :].rearrange("p (h n) -> p h n", h=KH)
        wrel = agg[:, 0:KH * R * F].rearrange("p (h r o) -> p h r o", h=KH, r=R)
        raw = agg[:, KH * R * F:KH * R * F + 4096].rearrange("p (a b e) -> p a b e", a=4, b=2)
        rows = sb("rows", [P, 2, R * F])
        ring = rows[:, :, :].rearrange("p u (s f) -> p (u s) f", f=F)
        w1s = sb("w1s", [P, EXP, KH, F])
        w2s = sb("w2s", [P, EXP, KH, F])
        b2s = sb("b2s", [EXP, F])
        ident = sb("ident", [P, P])
        small = sb("small", [P, F])
        smallT = sb("smallT", [P, KH, P])
        gateT = smallT[:, :, 0:R]
        routerT = smallT[:, :, 32:32 + EXP]
        hn = sb("hn", [P, 2, F])
        hT = sb("hT", [P, 2, KH, P])
        gate = sb("gate", [P, 2, R])
        stat = sb("stat", [P, 2, 6])
        mv = sb("mv", [P, 2, 2])
        var = sb("var", [P, 2])
        ybits = sb("ybits", [P, 2], I32)
        rstd = sb("rstd", [P, 2])
        tmp = sb("tmp", [P, 2])
        keyT = sb("keyT", [P, GROUPS, 4], I32)
        relT = sb("relT", [P, GROUPS, 4])
        wT = sb("wT", [P, GROUPS, 4])
        idx = sb("idx", [P, 2, GPI * 4], I32)
        iotai = sb("iotai", [P, WIN], I32)
        iota = sb("iota", [P, WIN])
        S = sb("S", [P, SLOTS, 4, WIN])                
        red = sb("red", [P, 2])
        span = sb("span", [P, 2, 2])
        acc = sb("acc", [P, 2, F])
        grow = acc[0:1, :, :].rearrange("o u f -> o (u f)").rearrange("o (g k) -> o g k", k=2)
        scan = sb("scan", [1, 2, 64])
        half = sb("half", [1, 2, GPI // 2 * ROUNDS])
        tab = sb("tab", [1, ROUNDS, 4 + GPI], I32)
        aggS = hT[:, :, :, :].rearrange("p u h q -> p (u h q)").rearrange("p (h n) -> p h n", h=KH)
        tokS = hn
        xT = sb("xT", [P, KH, BATCH])
        hid = sb("hid", [P, 2, KH, BATCH])
        lg = sb("lg", [P, 2, EXP])
        pr = sb("pr", [P, 2, EXP])
        rank = sb("rank", [P, 2, EXP])
        comb = sb("comb", [P, 2, EXP])
        cmp = sb("cmp", [P, 2, EXP, EXP])
        cmp2 = sb("cmp2", [P, 2, EXP, EXP])
        lower = sb("lower", [P, EXP, EXP])
        col = sb("col", [P, 2])
        top = sb("top", [P, 2])
        combT = sb("combT", [EXP, 2, P])
        bank = [ctx.enter_context(nc.psum_tensor(f"bank{n}", [P, 512], FP32)) for n in range(8)]

        x_in = [sem(f"x_in{n}") for n in range(5)]
        small_in, b2_in, raw_in, grow_in = sem("small_in"), sem("b2_in"), sem("raw_in"), sem("grow_in")
        w_in = [sem(f"w_in{n}") for n in range(8)]
        exp_in = sem("exp_in")
        table_out = [sem("table_out0"), sem("table_out1")]
        rows_free = sem("rows_free")
        pool_chain = sem("pool_chain")
        ident_ok, small_zero, raw_zero, edges_ok, tabs_ok = (
            sem("ident_ok"), sem("small_zero"), sem("raw_zero"), sem("edges_ok"), sem("tabs_ok"))
        span_ok2 = sem("span_ok2")
        span_ok, span_out, tab_chain = sem("span_ok"), sem("span_out"), sem("tab_chain")
        iota_ok = sem("iota_ok")
        small_tr, small_ok = sem("small_tr"), sem("small_ok")
        res_zero = sem("res_zero")
        ln_chain, ln_pair = sem("ln_chain"), sem("ln_pair")
        tr_done, hT_ok, gate_mm, gate_ok = sem("tr_done"), sem("hT_ok"), sem("gate_mm"), sem("gate_ok")
        mm_done, evac_act, evac_dve = sem("mm_done"), sem("evac_act"), sem("evac_dve")
        edge_tr, edge_ev = sem("edge_tr"), [sem("edge_act"), sem("edge_dve")]
        agg_zero = sem("agg_zero")
        turn_free = sem("turn_free")
        idx_ok = sem("idx_ok")
        gathered = [sem(f"gathered{r}") for r in range(GPI)]
        S_ok, seg_mm, added, shifted = sem("S_ok"), sem("seg_mm"), sem("added"), sem("shifted")
        relu_ok, agg_tr, tok_chain, tok_ok, tok_tr, xT_ok = (
            sem("relu_ok"), sem("agg_tr"), sem("tok_chain"), sem("tok_ok"), sem("tok_tr"), sem("xT_ok"))
        logit_mm, exp_ready, exp_ok, route_chain = (
            sem("logit_mm"), sem("exp_ready"), sem("exp_ok"), sem("route_chain"))
        comb_ok, top_ok = sem("comb_ok"), sem("top_ok")
        comb_tr, combT_ok, bias_mm, acc_done = sem("comb_tr"), sem("combT_ok"), sem("bias_mm"), sem("acc_done")
        h_mm, hid_ok, y_mm, y_added = sem("h_mm"), sem("hid_ok"), sem("y_mm"), sem("y_added")
        out_done, acc_free = sem("out_done"), sem("acc_free")
        hold = sem("hold")

        def round_numbers(engine, i, registers):
            engine.load(registers, tab[0:1, bass.ds(i, 1), 0:len(registers)].rearrange("o r k -> o (r k)"))
            return (engine.snap(registers[0], min_val=0, max_val=NPAD // WIN),
                    engine.snap(registers[1], min_val=0, max_val=BATCHES),
                    engine.snap(registers[2], min_val=0, max_val=BATCHES))

        block = ctx.enter_context(nc.Block())

        @block.sync
        def _(sp):
            def load_x(n, t0, t1):
                sp.dma_start(res[:, t0:t1, :], x[t0 * P:t1 * P, :].rearrange("(t p) f -> p t f", p=P)
                             ).then_inc(x_in[n], 16)
            load_x(0, 0, 2)
            sp.wait_ge(small_zero, 1)
            sp.dma_start(small[0:R, :], ggate.rearrange("r f o -> r (f o)")).then_inc(small_in, 16)
            sp.dma_start(small[32:32 + EXP, :], router).then_inc(small_in, 16)
            sp.dma_start(small[64:64 + EXP * KH, 0:P], b1.rearrange("e (h p) -> (e h) p", p=P)).then_inc(small_in, 16)
            for n in range(8):
                for h in range(KH):
                    sp.dma_start(wrel[:, h, 2 * n:2 * n + 2, :],
                                 gw[2 * n:2 * n + 2, h * P:(h + 1) * P, :].rearrange("r p o -> p r o")
                                 ).then_inc(w_in[n], 16)
                if n == 0:
                    load_x(1, 2, 14)
            sp.wait_ge(raw_zero, 1)
            for a, arr in enumerate((src, dst, etype, eweight)):
                out_dt = FP32 if a == 3 else I32
                flat = arr if a < 3 else arr.rearrange("e o -> (e o)")
                view = raw[:, a, :, :] if a == 3 else raw[:, a, :, :].bitcast(I32)
                sp.dma_start(view[:, 0, :], flat[0:P * GROUP].rearrange("(q e) -> q e", q=P)).then_inc(raw_in, 16)
                sp.dma_start(view[0:FULL - P, 1, :], flat[P * GROUP:FULL * GROUP].rearrange("(q e) -> q e", e=GROUP)
                             ).then_inc(raw_in, 16)
                sp.dma_start(view[FULL - P:FULL - P + 1, 1, 0:REST], flat[FULL * GROUP:E].rearrange("(q e) -> q e", q=1)
                             ).then_inc(raw_in, 16)
            load_x(2, 14, 31)
            load_x(3, 31, TILES - 1)
            sp.wait_ge(res_zero, 1)
            sp.dma_start(res[0:LAST_ROWS, TILES - 1, :], x[(TILES - 1) * P:N, :]).then_inc(x_in[4], 16)
            sp.dma_start(b2s[:, :], b2).then_inc(b2_in, 16)

            def write_half(slot, q2, node, count, rows_n=P):
                sp.wait_ge(evac_act, count)
                sp.wait_ge(evac_dve, count)
                span_ = R * F // 2
                dstv = table[bass.ds(node * R, rows_n * R), :].rearrange("(n r) f -> n (r f)", r=R)
                sp.dma_start(dstv[:, q2 * span_:(q2 + 1) * span_], rows[0:rows_n, slot, q2 * span_:(q2 + 1) * span_]
                             ).then_inc(table_out[slot], 16)

            def write_tiles(i0, i1):
                with sp.Fori(i0, i1) as i:
                    write_half(0, 0, i * (2 * P), i * 8 + 4)
                    write_half(0, 1, i * (2 * P), i * 8 + 6)
                    write_half(1, 0, i * (2 * P) + P, i * 8 + 8)
                    sp.wait_ge(table_out[0], i * 32 + 32)
                    sp.sem_inc(rows_free, 1)
                    write_half(1, 1, i * (2 * P) + P, i * 8 + 10)
                    sp.wait_ge(table_out[1], i * 32 + 32)
                    sp.sem_inc(rows_free, 1)

            sp.sem_inc(rows_free, 2)
            write_tiles(0, THIRD[1])
            for w_t, w_s in ((w1, w1s), (w2, w2s)):
                for h in range(KH):
                    sp.dma_start(w_s[:, :, h, :], w_t[:, h * P:(h + 1) * P, :].rearrange("e p o -> p e o")
                                 ).then_inc(exp_in, 16)
            write_tiles(THIRD[1], TILES // 2)
            write_half(0, 0, (TILES - 1) * P, (TILES - 1) * 4 + 4, LAST_ROWS)
            write_half(0, 1, (TILES - 1) * P, (TILES - 1) * 4 + 6, LAST_ROWS)

            sent = sp.alloc_register("sent")
            sp.reg_mov(sent, 0)
            row = [sp.alloc_register(f"row{k}") for k in range(4)]
            sp.sem_inc(acc_free, 1)
            sp.wait_ge(tabs_ok, 1)
            with sp.Fori(0, ROUNDS) as i:
                _, lo, hi = round_numbers(sp, i, row)
                first = sp.snap((lo < 1) * 1 + lo, min_val=0, max_val=BATCHES)
                with sp.If(first < hi):
                    with sp.Fori(first, hi):
                        b = sp.snap(sent, min_val=0, max_val=BATCHES - 2)
                        sp.wait_ge(acc_done, b + 2)
                        sp.dma_start(out[bass.ds(b * BATCH, BATCH), :].rearrange("(u p) f -> p u f", p=P),
                                     acc[:, :, :]).then_inc(out_done, 16)
                        sp.wait_ge(out_done, b * 16 + 16)
                        sp.sem_inc(acc_free, 1)
                        sp.reg_add(sent, sent, 1)
            sp.wait_ge(acc_done, BATCHES + 1)
            left = N - (BATCHES - 1) * BATCH
            for u in range(2):
                n0 = (BATCHES - 1) * BATCH + u * P
                n1 = min(n0 + P, N)
                if n1 > n0:
                    sp.dma_start(out[n0:n1, :], acc[0:n1 - n0, u, :]).then_inc(out_done, 16)
            sp.wait_ge(out_done, 16 * (BATCHES - 1) + 16 * (-(-left // P)))

        @block.gpsimd
        def _(pool):
            chain = Chain(pool, pool_chain)
            chain(pool.memset(small[:, :], 0.0))
            pool.sem_inc(small_zero, 1)
            chain(pool.memset(ident[:, :], 0.0))
            pool.affine_select(out=ident[:, :], in_=ident[:, :], compare_op=ALU.not_equal, fill=1.0, base=0,
                               pattern=[[-1, P]], channel_multiplier=1).then_inc(ident_ok, 1)
            pool.memset(raw[:, 0, 1, :].bitcast(I32), 0)
            pool.memset(raw[:, 1, 1, :].bitcast(I32), NPAD - 1)
            pool.memset(raw[:, 2, 1, :].bitcast(I32), 0)
            pool.memset(raw[:, 3, 1, :], 0.0).then_inc(raw_zero, 1)
            pool.iota(iotai[:, :], pattern=[[1, WIN]], base=0, channel_multiplier=0).then_inc(iota_ok, 1)
            pool.wait_ge(iota_ok, 1)
            pool.tensor_copy(iota[:, :], iotai[:, :]).then_inc(iota_ok, 1)
            chain(pool.memset(lower[:, :, :], 1.0))
            chain(pool.affine_select(out=lower[:, :, :], in_=lower[:, :, :], compare_op=ALU.is_gt, fill=0.0, base=0,
                                     pattern=[[1, EXP], [-1, EXP]], channel_multiplier=0))
            pool.wait_ge(span_ok, 1)
            chain(pool.tensor_copy(raw[:, 1, :, :], raw[:, 1, :, :].bitcast(I32)))
            for b in range(2):
                chain(pool.tensor_scalar(raw[:, 1, b, :], raw[:, 1, b, :], span[:, b, 0:1], None, ALU.subtract))
            chain(pool.tensor_scalar(raw[:, 0, :, :], raw[:, 0, :, :].bitcast(I32), float(R), None, ALU.mult))
            chain(pool.tensor_copy(raw[:, 2, :, :], raw[:, 2, :, :].bitcast(I32)))
            pool.tensor_tensor(raw[:, 0, :, :], raw[:, 0, :, :], raw[:, 2, :, :], ALU.add
                               ).then_inc(edges_ok, 1)
            pool.dma_start(group_dram.rearrange("(b q) k -> q b k", q=P), span[:, :, :]).then_inc(span_out, 16)
            pool.wait_ge(span_out, 16)
            pool.dma_start(grow[:, :, :], group_dram.rearrange("(o g) k -> o g k", o=1)).then_inc(grow_in, 16)

            pool.wait_ge(edge_ev[0], 3)
            pool.wait_ge(edge_ev[1], 3)
            pool.wait_ge(table_out[0], 32 * (TILES // 2 + 1))
            pool.wait_ge(table_out[1], 32 * (TILES // 2))
            pool.sem_inc(hold, 1)
            passes = pool.alloc_register("passes")
            pool.reg_mov(passes, 0)
            with pool.Fori(0, ROUNDS // 2) as i:
                for h in range(2):
                    extra = pool.value_load(tab[0:1, bass.ds(i * 2 + h, 1), 0:1].rearrange("o r k -> o (r k)"),
                                            min_val=0, max_val=NPAD // WIN)
                    p = pool.snap(passes, min_val=0, max_val=1 << 20)
                    pool.wait_ge(seg_mm, p * GPI + 1)
                    pool.sem_inc(hold, 1)
                    pool.tensor_copy(idx[:, h, :], keyT[:, bass.ds(i * (2 * GPI) + h * GPI, GPI), :].rearrange("p g j -> p (g j)")
                                     ).then_inc(idx_ok, 1)
                    pool.wait_ge(idx_ok, i * 2 + (h + 1))
                    for r in range(GPI):
                        pool.wait_ge(seg_mm, p * GPI + (r + 1))
                        pool.sem_inc(turn_free, 1)
                        for j in range(4):
                            pool.indirect_dma_start(
                                out=ring[:, r * 4 + j, :], out_offset=None, in_=table[:, :],
                                in_offset=bass.IndirectOffsetOnAxis(ap=idx[:, h, r * 4 + j:r * 4 + j + 1], axis=0),
                            ).then_inc(gathered[r], 16)
                    pool.reg_add(passes, passes, extra + 1)

        @block.scalar
        def _(act):
            act.sem_inc(evac_act, 2)
            act.sem_inc(hT_ok, 2)
            act.sem_inc(gate_ok, 1)
            act.wait_ge(small_tr, 1)
            act.activation(smallT[:, :, :], bank[7][:, 0:KH * P].rearrange("p (h q) -> p h q", h=KH), ACT.Copy
                           ).then_inc(small_ok, 1)

            def copy_hT(u, t):
                act.wait_ge(tr_done, t + 3)
                act.wait_ge(mm_done, t * 8 + 8)
                act.activation(hT[:, u, :, :], bank[4 + u][:, 0:KH * P].rearrange("p (h q) -> p h q", h=KH), ACT.Copy
                               ).then_inc(hT_ok, 1)

            def gates_and_rows(u, t):
                act.wait_ge(gate_mm, t + 1)
                act.wait_ge(rows_free, t + 1)
                act.activation(gate[:, u, :], bank[6][:, 0:R], ACT.Sigmoid).then_inc(gate_ok, 1)
                act.wait_ge(gate_ok, t + 2)
                for k in range(4):
                    q = 2 * k
                    act.wait_ge(mm_done, t * 8 + (q + 17))
                    for r in range(2):
                        ins = act.activation(rows[:, u, (2 * q + r) * F:(2 * q + r + 1) * F],
                                             bank[q % 4][:, r * F:(r + 1) * F], ACT.Copy,
                                             scale=gate[:, u, 2 * q + r:2 * q + r + 1])
                    ins.then_inc(evac_act, 1)

            copy_hT(0, 0)

            def part1(i0, i1):
                with act.Fori(i0, i1) as i:
                    copy_hT(1, i * 2 + 1)
                    gates_and_rows(0, i * 2)
                    copy_hT(0, i * 2 + 2)
                    gates_and_rows(1, i * 2 + 1)

            part1(0, THIRD[1])
            for n, dst_ in ((0, keyT), (2, relT), (4, wT)):
                act.wait_ge(edge_tr, n + 1)
                act.activation(dst_[:, 0:P, :].rearrange("p g j -> p j g"),
                               bank[7][:, :].rearrange("p (j g) -> p j g", j=4), ACT.Copy).then_inc(edge_ev[0], 1)
            part1(THIRD[1], TILES // 2)
            gates_and_rows(0, TILES - 1)

            act.sem_inc(hid_ok, 2)
            act.wait_ge(tabs_ok, 1)
            done = act.alloc_register("batches")
            act.reg_mov(done, 0)
            row = [act.alloc_register(f"row{k}") for k in range(4)]
            mixed = act.alloc_register("mixed")
            act.reg_mov(mixed, 0)

            def experts(b):
                for e in range(EXP):
                    act.wait_ge(h_mm, b * EXP + (e + 1))
                    act.wait_ge(y_mm, b * EXP + (e + 1))
                    for h in range(KH):
                        ins = act.activation(hid[:, e % 2, h, :], bank[2 + e % 2][:, h * BATCH:(h + 1) * BATCH],
                                             ACT.Gelu, bias=smallT[:, 0, 64 + e * KH + h:65 + e * KH + h])
                    ins.then_inc(hid_ok, 1)

            with act.Fori(0, ROUNDS) as i:
                _, lo, hi = round_numbers(act, i, row)
                with act.If(lo < hi):
                    with act.Fori(lo, hi):
                        f = act.snap(done, min_val=0, max_val=BATCHES - 1)
                        with act.If(f > 0):
                            experts(act.snap(mixed, min_val=0, max_val=BATCHES - 2))
                            act.reg_add(mixed, mixed, 1)
                        act.wait_ge(tok_tr, f + 1)
                        act.activation(xT[:, :, :], bank[6][:, :].rearrange("p (h n) -> p h n", h=KH), ACT.Copy
                                       ).then_inc(xT_ok, 1)
                        act.wait_ge(exp_ready, f + 1)
                        act.activation(pr[:, :, :], lg[:, :, :], ACT.Exp).then_inc(exp_ok, 1)
                        act.reg_add(done, done, 1)
            experts(BATCHES - 1)

        @block.vector
        def _(dve):
            dve.sem_inc(evac_dve, 2)
            dve.memset(res[:, TILES - 1:2 * BATCHES, :], 0.0).then_inc(res_zero, 1)

            def rstd_of(chain, width):
                v, y, t = var[:, 0:width], rstd[:, 0:width], tmp[:, 0:width]
                chain(dve.tensor_scalar(v, mv[:, 0:width, 1], EPS, None, ALU.add))
                chain(dve.tensor_scalar(ybits[:, 0:width], v.bitcast(I32), 1, None, ALU.arith_shift_right))
                chain(dve.tensor_scalar(y.bitcast(I32), ybits[:, 0:width], -1.0, RSQRT_MAGIC, ALU.mult, ALU.add))
                for _ in range(3):
                    chain(dve.tensor_tensor(t, y, y, ALU.mult))
                    chain(dve.tensor_tensor(t, t, v, ALU.mult))
                    chain(dve.tensor_scalar(t, t, -0.5, 1.5, ALU.mult, ALU.add))
                    chain(dve.tensor_tensor(y, y, t, ALU.mult))

            def stats(chain, tile):
                for u in range(2):
                    dve.sem_inc(hold, 1)
                    chain(dve.bn_stats(stat[:, u, :], tile(u)))
                for u in range(2):
                    dve.sem_inc(hold, 1)
                    chain(dve.bn_aggr(mv[:, u, :], stat[:, u, :]))
                rstd_of(chain, 2)

            def norm_pair(chain, t):
                for u in range(2):
                    dve.wait_ge(tr_done, t + (1 + u))
                    dve.sem_inc(hold, 1)
                    dve.tensor_scalar(hn[:, u, :], res[:, bass.ds(t + u, 1), :].rearrange("p o f -> p (o f)"),
                                      mv[:, u, 0:1], rstd[:, u:u + 1], ALU.subtract, ALU.mult).then_inc(ln_pair, 1)

            def rows_of(t):
                return lambda u: res[:, bass.ds(t + u, 1), :].rearrange("p o f -> p (o f)")

            def evacuate(u, t, k):
                q = 2 * k + 1
                dve.wait_ge(mm_done, t * 8 + (q + 17))
                dve.tensor_tensor(rows[:, u, 2 * q * F:(2 * q + 2) * F].rearrange("p (r f) -> p r f", r=2),
                                  bank[q % 4][:, :].rearrange("p (r f) -> p r f", r=2),
                                  gate[:, u, 2 * q:2 * q + 2].unsqueeze(2).to_broadcast([P, 2, F]), ALU.mult
                                  ).then_inc(evac_dve, 1)

            LINKS = 4 + 3 + 12
            dve.wait_ge(x_in[0], 16)
            first = Chain(dve, ln_chain)
            stats(first, rows_of(0))
            norm_pair(None, 0)
            assert first.n == LINKS

            def part1(i0, i1):
                with dve.Fori(i0, i1) as i:
                    for u in range(2):
                        t = i * 2 + u
                        dve.wait_ge(gate_ok, t + 2)
                        dve.wait_ge(rows_free, t + 1)
                        for k in range(4):
                            evacuate(u, t, k)
                            if u == 0 and k == 0:
                                c = Chain(dve, ln_chain, (i + 1) * LINKS)
                                dve.wait_ge(ln_pair, i * 2 + 2)
                                stats(c, rows_of(i * 2 + 2))
                                assert c.n == LINKS
                            if u == 0 and k == 1:
                                norm_pair(None, i * 2 + 2)

            dve.wait_ge(x_in[1], 16)
            part1(0, THIRD[0])
            dve.wait_ge(raw_in, 12 * 16)
            dve.tensor_reduce(span[:, :, 0], raw[:, 1, :, :].bitcast(I32), AX.X, ALU.min).then_inc(span_ok2, 1)
            dve.tensor_reduce(red[:, :], raw[:, 1, :, :].bitcast(I32), AX.X, ALU.max).then_inc(span_ok2, 1)
            dve.wait_ge(span_ok2, 2)
            dve.tensor_tensor(span[:, :, 1], red[:, :], span[:, :, 0], ALU.subtract).then_inc(span_ok, 1)
            dve.wait_ge(x_in[2], 16)
            dve.wait_ge(x_in[3], 16)
            part1(THIRD[0], THIRD[1])
            chain = Chain(dve, tab_chain)
            dve.wait_ge(grow_in, 16)
            lows, spans = grow[0:1, 0:GROUPS, 0], grow[0:1, 0:GROUPS, 1]
            chain(dve.memset(tab[0:1, :, :], 0))
            chain(dve.tensor_copy(tab[0:1, :, 4:4 + GPI], lows.rearrange("o (r g) -> o r g", g=GPI)))

            def over_groups(v, k, op):
                a = v.rearrange("o (r g) -> o r g", g=GPI)
                n = GPI // 2
                dst_ = half[0:1, k, :].rearrange("o (r g) -> o r g", g=n)
                chain(dve.tensor_tensor(dst_, a[:, :, 0:n], a[:, :, n:2 * n], op))
                while n > 1:
                    n //= 2
                    chain(dve.tensor_tensor(dst_[:, :, 0:n], dst_[:, :, 0:n], dst_[:, :, n:2 * n], op))
                return dst_[:, :, 0]
            widest = over_groups(spans, 0, ALU.max)
            chain(dve.tensor_scalar(tab[0:1, :, 0], widest, 1.0 / WIN, 0.5 / WIN - 0.5, ALU.mult, ALU.add))
            lowest = over_groups(lows, 1, ALU.min)
            chain(dve.memset(scan[0:1, :, :], float(NPAD)))
            chain(dve.tensor_copy(scan[0:1, 0, 0:ROUNDS - 1], lowest[:, 1:ROUNDS]))
            step, k = 1, 0
            while step < ROUNDS:
                chain(dve.tensor_tensor(scan[0:1, 1 - k, 0:ROUNDS], scan[0:1, k, 0:ROUNDS],
                                         scan[0:1, k, step:step + ROUNDS], ALU.min))
                step, k = 2 * step, 1 - k
            for at, count, c in ((0, ROUNDS, 2), (1, ROUNDS - 1, 1)):
                chain(dve.tensor_scalar(tab[0:1, at:ROUNDS, c], scan[0:1, k, 0:count], 1.0 / BATCH,
                                        0.5 / BATCH - 0.5, ALU.mult, ALU.add))
            dve.sem_inc(tabs_ok, 1)
            for n, dst_ in ((1, keyT), (3, relT), (5, wT)):
                dve.wait_ge(edge_tr, n + 1)
                dve.tensor_copy(dst_[:, P:GROUPS, :].rearrange("p g j -> p j g"),
                                bank[6][:, :].rearrange("p (j g) -> p j g", j=4)[:, :, 0:GROUPS - P]).then_inc(edge_ev[1], 1)
            dve.wait_ge(x_in[4], 16)
            part1(THIRD[1], TILES // 2)
            dve.wait_ge(gate_ok, TILES + 1)
            dve.wait_ge(rows_free, TILES)
            for k in range(4):
                evacuate(0, TILES - 1, k)

            dve.wait_ge(mm_done, 8 * TILES + 16)
            dve.memset(agg[:, :], 0.0).then_inc(agg_zero, 1)
            dve.sem_inc(added, 2)
            dve.sem_inc(shifted, 1)
            dve.sem_inc(y_added, 2)
            dve.sem_inc(acc_done, 1)
            dve.wait_ge(tabs_ok, 1)
            dve.wait_ge(iota_ok, 2)
            dve.wait_ge(edge_ev[0], 3)
            dve.wait_ge(edge_ev[1], 3)
            dve.wait_ge(agg_zero, 1)
            passes = dve.alloc_register("passes")
            done = dve.alloc_register("batches")
            base = dve.alloc_register("base")
            row = [dve.alloc_register(f"row{k}") for k in range(4 + GPI)]
            dve.reg_mov(passes, 0)
            dve.reg_mov(done, 0)
            mixed = dve.alloc_register("mixed")
            dve.reg_mov(mixed, 0)

            def experts(b):
                dve.wait_ge(acc_free, b + 1)
                for e in range(EXP):
                    dve.wait_ge(y_mm, b * EXP + (e + 3))
                    for u in range(2):
                        dve.wait_ge(y_added, b * (2 * EXP) + (2 * e + u + 1))
                        before = rows_of(b * 2)(u) if e == 0 else acc[:, u, :]
                        if e == 0:
                            dve.sem_inc(hold, 1)
                        dve.scalar_tensor_tensor(acc[:, u, :], bank[4 + e % 2][:, u * F:(u + 1) * F],
                                                 comb[:, u, e:e + 1], before, ALU.mult, ALU.add
                                                 ).then_inc(y_added, 1)
                dve.wait_ge(bias_mm, b + 1)
                dve.wait_ge(y_added, b * (2 * EXP) + (2 * EXP + 2))
                dve.tensor_tensor(acc[:, :, :], acc[:, :, :], bank[7][:, :].rearrange("p (u f) -> p u f", u=2), ALU.add
                                  ).then_inc(acc_done, 1)

            TOK_LINKS = 1 + LINKS
            ROUTE_LINKS = 2 + 6 + 5

            def tokens(f):
                c = Chain(dve, tok_chain, f * TOK_LINKS)
                pair = res[:, bass.ds(f * 2, 2), :]
                dve.wait_ge(agg_tr, f + 2)
                chain_in = dve.tensor_tensor(pair, bank[6][:, :].rearrange("p (u f) -> p u f", u=2), pair, ALU.add)
                c(chain_in)
                stats(c, rows_of(f * 2))
                for u in range(2):
                    dve.tensor_scalar(tokS[:, u, :], rows_of(f * 2)(u), mv[:, u, 0:1], rstd[:, u:u + 1],
                                      ALU.subtract, ALU.mult).then_inc(tok_ok, 1)
                assert c.n == TOK_LINKS
                dve.wait_ge(tok_ok, f * 3 + 2)
                dve.tensor_tensor(pair, pair, tokS[:, :, :], ALU.add).then_inc(tok_ok, 1)

            def shift_logits(f):
                dve.wait_ge(logit_mm, f + 1)
                L = bank[7][:, 0:2 * EXP].rearrange("p (u e) -> p u e", u=2)
                dve.tensor_reduce(top[:, :], L, AX.X, ALU.max).then_inc(top_ok, 1)
                dve.wait_ge(top_ok, f + 1)
                dve.tensor_tensor(lg[:, :, :], L, top[:, :].unsqueeze(2).to_broadcast([P, 2, EXP]), ALU.subtract
                                  ).then_inc(exp_ready, 1)

            def route(f):
                c = Chain(dve, route_chain, f * ROUTE_LINKS)
                dve.wait_ge(exp_ok, f + 1)
                c(dve.tensor_reduce(col[:, :], pr[:, :, :], AX.X, ALU.add))
                c(dve.reciprocal(col[:, :], col[:, :]))
                c(dve.tensor_tensor(pr[:, :, :], pr[:, :, :], col[:, :].unsqueeze(2).to_broadcast([P, 2, EXP]), ALU.mult))
                pj = pr[:, :, :].unsqueeze(2).to_broadcast([P, 2, EXP, EXP])
                pe_ = pr[:, :, :].unsqueeze(3).to_broadcast([P, 2, EXP, EXP])
                low_ = lower[:, :, :].unsqueeze(1).to_broadcast([P, 2, EXP, EXP])
                c(dve.tensor_tensor(cmp[:, :, :, :], pj, pe_, ALU.is_gt))
                c(dve.tensor_tensor(cmp2[:, :, :, :], pj, pe_, ALU.is_equal))
                c(dve.tensor_tensor(cmp2[:, :, :, :], cmp2[:, :, :, :], low_, ALU.mult))
                c(dve.tensor_tensor(cmp[:, :, :, :], cmp[:, :, :, :], cmp2[:, :, :, :], ALU.add))
                c(dve.tensor_reduce(rank[:, :, :], cmp[:, :, :, :], AX.X, ALU.add))
                c(dve.scalar_tensor_tensor(pr[:, :, :], rank[:, :, :], 1.5, pr[:, :, :], ALU.is_lt, ALU.mult))
                c(dve.tensor_reduce(col[:, :], pr[:, :, :], AX.X, ALU.add))
                c(dve.tensor_scalar(col[:, :], col[:, :], 1e-12, None, ALU.max))
                c(dve.reciprocal(col[:, :], col[:, :]))
                dve.wait_ge(y_added, f * (2 * EXP) + 2)
                dve.wait_ge(comb_tr, f + 1)
                c(dve.tensor_tensor(comb[:, :, :], pr[:, :, :], col[:, :].unsqueeze(2).to_broadcast([P, 2, EXP]), ALU.mult))
                assert c.n == ROUTE_LINKS, c.n
                dve.sem_inc(comb_ok, 1)

            def combT_copy(b):
                dve.wait_ge(comb_tr, b + 2)
                dve.tensor_copy(combT[:, :, :], bank[7][0:EXP, 0:2 * P].rearrange("e (u p) -> e u p", u=2)
                                ).then_inc(combT_ok, 1)

            with dve.Fori(0, ROUNDS) as i:
                extra, lo, hi = round_numbers(dve, i, row)
                with dve.Fori(0, extra + 1) as w:
                    p = dve.snap(passes, min_val=0, max_val=1 << 20)
                    for r in range(GPI + 1):
                        if r < GPI:
                            g = i * GPI + r
                            dve.wait_ge(shifted, p + 1)
                            dve.wait_ge(seg_mm, p * GPI + (r + 1 + GPI - SLOTS))
                            dve.sem_inc(hold, 1)
                            for j in range(4):
                                ins = dve.tensor_scalar(S[:, r % SLOTS, j, :], iota[:, :],
                                                        relT[:, bass.ds(g, 1), j:j + 1].rearrange("p o k -> p (o k)"),
                                                        wT[:, bass.ds(g, 1), j:j + 1].rearrange("p o k -> p (o k)"),
                                                        ALU.is_equal, ALU.mult)
                            ins.then_inc(S_ok, 1)
                        if r >= 1:
                            s = r - 1
                            low_ = dve.snap(row[4 + s], min_val=0, max_val=NPAD - 1)
                            dve.reg_alu(base, low_ + w * WIN, NPAD, ALU.min)
                            to = dve.snap(base, min_val=0, max_val=NPAD)
                            dve.wait_ge(seg_mm, p * GPI + (s + GPI + 1))
                            dve.wait_ge(added, p * GPI + (s + 2))
                            window = aggv[:, :, bass.ds(to, WIN)]
                            dve.tensor_tensor(window, window,
                                              bank[s % 2][:, 0:KH * WIN].rearrange("p (h n) -> p h n", h=KH), ALU.add
                                              ).then_inc(added, 1)
                    dve.wait_ge(S_ok, p * GPI + GPI)
                    dve.sem_inc(hold, 1)
                    moved = relT[:, bass.ds(i * GPI, GPI), :]
                    dve.tensor_scalar(moved, moved, float(WIN), None, ALU.subtract).then_inc(shifted, 1)
                    dve.reg_add(passes, passes, 1)
                with dve.If(lo < hi):
                    with dve.Fori(lo, hi):
                        f = dve.snap(done, min_val=0, max_val=BATCHES - 1)
                        dve.wait_ge(added, dve.snap(passes, min_val=0, max_val=1 << 20) * GPI + 2)
                        dve.wait_ge(agg_tr, f + 1)
                        dve.sem_inc(hold, 1)
                        dve.tensor_scalar(aggS[:, :, :], aggv[:, :, bass.ds(f * BATCH, BATCH)], 0.0, None, ALU.max
                                          ).then_inc(relu_ok, 1)
                        with dve.If(f > 0):
                            route(dve.snap(mixed, min_val=0, max_val=BATCHES - 2))
                        tokens(f)
                        with dve.If(f > 0):
                            combT_copy(dve.snap(mixed, min_val=0, max_val=BATCHES - 2))
                            experts(dve.snap(mixed, min_val=0, max_val=BATCHES - 2))
                            dve.reg_add(mixed, mixed, 1)
                        shift_logits(f)
                        dve.reg_add(done, done, 1)
            route(BATCHES - 1)
            combT_copy(BATCHES - 1)
            experts(BATCHES - 1)

        @block.tensor
        def _(pe):
            pe.wait_ge(ident_ok, 1)
            pe.wait_ge(small_in, 48)
            for h in range(KH):
                ins = pe.transpose(bank[7][:, h * P:(h + 1) * P], small[:, h * P:(h + 1) * P], ident[:, :])
            ins.then_inc(small_tr, 1)
            pe.sem_inc(tr_done, 2)
            pe.sem_inc(mm_done, 16)

            def transposes(u, t):
                pe.wait_ge(ln_pair, t + 1)
                pe.wait_ge(hT_ok, t + 1)
                for h in range(KH):
                    ins = pe.transpose(bank[4 + u][:, h * P:(h + 1) * P], hn[:, u, h * P:(h + 1) * P], ident[:, :])
                ins.then_inc(tr_done, 1)

            def messages(u, t):
                pe.wait_ge(hT_ok, t + 3)
                pe.wait_ge(gate_ok, t + 1)
                for h in range(KH):
                    ins = pe.matmul(bank[6][:, 0:R], hT[:, u, h, :], gateT[:, h, :], start=h == 0, stop=h == KH - 1)
                ins.then_inc(gate_mm, 1)
                for q in range(8):
                    pe.wait_ge(w_in[q], 32)
                    pe.wait_ge((evac_act, evac_dve)[q % 2], t * 4 + (q // 2 + 1))
                    for h in range(KH):
                        ins = pe.matmul(bank[q % 4][:, :], hT[:, u, h, :],
                                        wrel[:, h, 2 * q:2 * q + 2, :].rearrange("p r o -> p (r o)"),
                                        start=h == 0, stop=h == KH - 1)
                    ins.then_inc(mm_done, 1)

            transposes(0, 0)
            pe.wait_ge(small_ok, 1)

            def part1(i0, i1):
                with pe.Fori(i0, i1) as i:
                    transposes(1, i * 2 + 1)
                    messages(0, i * 2)
                    transposes(0, i * 2 + 2)
                    messages(1, i * 2 + 1)

            part1(0, THIRD[1])
            pe.wait_ge(edges_ok, 1)
            pe.wait_ge(gate_ok, 2 * THIRD[1] + 1)
            for n, a in enumerate((0, 0, 1, 1, 3, 3)):
                if n >= 2:
                    pe.wait_ge(edge_ev[n % 2], n // 2)
                for j in range(4):
                    ins = pe.transpose(bank[7 if n % 2 == 0 else 6][:, j * P:(j + 1) * P],
                                       raw[:, a, n % 2, j * P:(j + 1) * P], ident[:, :])
                ins.then_inc(edge_tr, 1)
            pe.wait_ge(edge_ev[0], 3)
            pe.wait_ge(edge_ev[1], 3)
            part1(THIRD[1], TILES // 2)
            messages(0, TILES - 1)

            pe.wait_ge(evac_act, 4 * TILES + 2)
            pe.wait_ge(evac_dve, 4 * TILES + 2)
            pe.wait_ge(exp_in, 64)
            pe.wait_ge(b2_in, 16)
            pe.wait_ge(tabs_ok, 1)
            pe.sem_inc(seg_mm, GPI)
            pe.sem_inc(agg_tr, 1)
            pe.sem_inc(y_mm, 2)
            pe.sem_inc(comb_tr, 1)
            passes = pe.alloc_register("passes")
            done = pe.alloc_register("batches")
            pe.reg_mov(passes, 0)
            pe.reg_mov(done, 0)
            row = [pe.alloc_register(f"row{k}") for k in range(4)]
            mixed = pe.alloc_register("mixed")
            pe.reg_mov(mixed, 0)

            def combine_T(b):
                pe.wait_ge(comb_ok, b + 1)
                for u in range(2):
                    ins = pe.transpose(bank[7][0:EXP, u * P:(u + 1) * P], comb[:, u, :], ident[:, :])
                ins.then_inc(comb_tr, 1)

            def hidden(b, e):
                pe.wait_ge(hid_ok, b * EXP + (e + 1))
                for m in range(KH):
                    for h in range(KH):
                        ins = pe.matmul(bank[2 + e % 2][:, m * BATCH:(m + 1) * BATCH],
                                        w1s[:, e, h, m * P:(m + 1) * P], xT[:, h, :], start=h == 0, stop=h == KH - 1)
                ins.then_inc(h_mm, 1)

            def first_experts(b):
                hidden(b, 0)
                hidden(b, 1)

            def experts(b):
                def project(e):
                    pe.wait_ge(hid_ok, b * EXP + (e + 3))
                    pe.wait_ge(y_added, b * (2 * EXP) + max(2 * e, 1))
                    for u in range(2):
                        for m in range(KH):
                            ins = pe.matmul(bank[4 + e % 2][:, u * F:(u + 1) * F], hid[:, e % 2, m, u * P:(u + 1) * P],
                                            w2s[:, e, m, :], start=m == 0, stop=m == KH - 1)
                    ins.then_inc(y_mm, 1)

                combine_T(b)
                for e in range(EXP):
                    project(e)
                    if e + 2 < EXP:
                        hidden(b, e + 2)
                    if e == 3:
                        pe.wait_ge(combT_ok, b + 1)
                        for u in range(2):
                            ins = pe.matmul(bank[7][:, u * F:(u + 1) * F], combT[:, u, :], b2s[:, :], start=True, stop=True)
                        ins.then_inc(bias_mm, 1)

            with pe.Fori(0, ROUNDS) as i:
                extra, lo, hi = round_numbers(pe, i, row)
                with pe.Fori(0, extra + 1):
                    p = pe.snap(passes, min_val=0, max_val=1 << 20)
                    for r in range(GPI):
                        pe.wait_ge(gathered[r], i * 64 + 64)
                        pe.wait_ge(S_ok, p * GPI + (r + 1))
                        pe.wait_ge(added, p * GPI + (r + 1))
                        for h in range(KH):
                            for j in range(4):
                                ins = pe.matmul(bank[r % 2][:, h * WIN:(h + 1) * WIN], ring[:, r * 4 + j, h * P:(h + 1) * P],
                                                S[:, r % SLOTS, j, :], start=j == 0, stop=j == 3)
                        ins.then_inc(seg_mm, 1)
                    pe.reg_add(passes, passes, 1)
                with pe.If(lo < hi):
                    with pe.Fori(lo, hi):
                        f = pe.snap(done, min_val=0, max_val=BATCHES - 1)
                        with pe.If(f > 0):
                            first_experts(pe.snap(mixed, min_val=0, max_val=BATCHES - 2))
                        pe.wait_ge(relu_ok, f + 1)
                        for u in range(2):
                            for h in range(KH):
                                ins = pe.transpose(bank[6][:, u * F + h * P:u * F + (h + 1) * P],
                                                   aggS[:, h, u * P:(u + 1) * P], ident[:, :])
                        ins.then_inc(agg_tr, 1)
                        with pe.If(f > 0):
                            experts(pe.snap(mixed, min_val=0, max_val=BATCHES - 2))
                            pe.reg_add(mixed, mixed, 1)
                        pe.wait_ge(tok_ok, f * 3 + 3)
                        for h in range(KH):
                            for u in range(2):
                                ins = pe.transpose(bank[6][:, h * BATCH + u * P:h * BATCH + (u + 1) * P],
                                                   tokS[:, u, h * P:(h + 1) * P], ident[:, :])
                        ins.then_inc(tok_tr, 1)
                        pe.wait_ge(xT_ok, f + 1)
                        pe.wait_ge(acc_done, f + 1)
                        for u in range(2):
                            for h in range(KH):
                                ins = pe.matmul(bank[7][:, u * EXP:(u + 1) * EXP], xT[:, h, u * P:(u + 1) * P],
                                                routerT[:, h, :], start=h == 0, stop=h == KH - 1)
                        ins.then_inc(logit_mm, 1)
                        pe.reg_add(done, done, 1)
            first_experts(BATCHES - 1)
            experts(BATCHES - 1)


_INPUTS = ["x", "src", "dst", "edge_type_16", "edge_weight1", "L0_gnn_weight", "L0_gnn_gate_weight",
           "L0_ffn_router_w", "L0_ffn_w1", "L0_ffn_b1", "L0_ffn_w2", "L0_ffn_b2"]


def kernel(**inputs):
    import numpy as np
    import concourse.bacc as bacc
    from concourse import mybir as mb
    from concourse.bass_utils import run_bass_kernel_spmd as run

    nc = bacc.Bacc("TRN2", target_bir_lowering=False, num_devices=1)
    arrays = {"in_" + k: np.ascontiguousarray(inputs[k]) for k in _INPUTS}
    args = [nc.dram_tensor(k, a.shape, mb.dt.from_np(a.dtype), kind="ExternalInput").ap() for k, a in arrays.items()]
    args.append(nc.dram_tensor("out", (N, F), mb.dt.float32, kind="ExternalOutput").ap())
    build(nc, *args)
    return run(nc, [arrays], core_ids=[0]).results[0]["out"]
```

```python
import concourse.bass as bass
from concourse import mybir
from contextlib import ExitStack

FP32 = mybir.dt.float32
F32R = mybir.dt.float32r
I32 = mybir.dt.int32
ALU = mybir.AluOpType
ACT = mybir.ActivationFunctionType
AX = mybir.AxisListType

N, E, R, F = 6250, 106250, 16, 256
P = 128
KH = F // P
EXP = 8
TILES = -(-N // P)
LAST_ROWS = N - (TILES - 1) * P
BATCH = 2 * P
BATCHES = -(-N // BATCH)
LAST_TILES = -(-(N - (BATCHES - 1) * BATCH) // P)
NPAD = BATCHES * BATCH
GROUP = 4 * P
GPI = 8
GROUPS = -(-E // GROUP)
ROUNDS = GROUPS // GPI
FULL = E // GROUP
REST = E - FULL * GROUP
WIN = 128
AGGW = NPAD + WIN
STAGE_AT = 18
THIRD = (8, 16)
BIAS_AT = 4
LEAD = 3
SLOTS = 4
EPS = 1e-5
RSQRT_MAGIC = float(0x5F3759DF)
ZERO = (R * F, KH * R * F, KH * R * F, KH * R * F + 4 * 2 * GROUP)
assert EXP == GPI
assert GROUPS == ROUNDS * GPI and P < FULL < 2 * P


class Chain:

    def __init__(self, engine, sem, base=0):
        self.engine, self.sem, self.base, self.n = engine, sem, base, 0

    def __call__(self, instruction):
        instruction.then_inc(self.sem, 1)
        self.n += 1
        self.engine.wait_ge(self.sem, self.base + self.n)


def build(nc, x, src, dst, etype, eweight, gw, ggate, router, w1, b1, w2, b2, out):
    assert GPI * 4 * F == R * F * 2
    table = nc.dram_tensor("message_table", (N * R, F), FP32, kind="Internal").ap()
    group_dram = nc.dram_tensor("group_numbers", (2 * P, 2), FP32, kind="Internal").ap()
    ctx = ExitStack()
    with ctx:
        def sb(name, shape, dt=FP32):
            return ctx.enter_context(nc.sbuf_tensor(name, shape, dt))

        def sem(name):
            return ctx.enter_context(nc.semaphore(name))

        res = sb("res", [P, 2 * BATCHES, F])
        staged = res[:, STAGE_AT:STAGE_AT + 4 * R // 2, :].rearrange("p (q h r) o -> p q h (r o)", q=R // 2, h=KH)
        with ExitStack() as first_part:
            def sb1(name, shape, dt=F32R):
                return first_part.enter_context(nc.sbuf_tensor(name, shape, dt))
            w_high = sb1("w_high", [P, R // 2, KH, 2 * F])
            raw = sb1("raw", [P, 4, 2, GROUP], FP32)
            hT = sb1("hT", [P, 2, KH, P])
            gate_high = sb1("gate_high", [P, KH, R])
            gate_low = sb1("gate_low", [P, KH, R])
            w_low = sb1("w_low", [P, R // 2, KH, 2 * F])
            hT_low = sb1("hT_low", [P, 2, KH, P])
        agg = sb("agg", [P, KH * AGGW])
        aggv = agg[:, :].rearrange("p (h n) -> p h n", h=KH)
        w1s = sb("w1s", [P, EXP, KH, F])
        w2s = sb("w2s", [P, EXP, KH, F])
        xT = sb("xT", [P, KH, BATCH])
        aggS = sb("aggS", [P, KH, BATCH])
        rows = sb("rows", [P, 2, R * F])
        ring = rows[:, :, :].rearrange("p u (s f) -> p (u s) f", f=F)
        b2s = sb("b2s", [EXP, F])
        ident = sb("ident", [P, P])
        small = sb("small", [P, F])
        smallT = sb("smallT", [P, KH, P])
        routerT = smallT[:, :, 32:32 + EXP]
        hn = sb("hn", [P, 2, F])
        gate = sb("gate", [P, 2, R])
        stat = sb("stat", [P, 2, 6])
        mv = sb("mv", [P, 2, 2])
        var = sb("var", [P, 2])
        ybits = sb("ybits", [P, 2], I32)
        rstd = sb("rstd", [P, 2])
        tmp = sb("tmp", [P, 2])
        keyT = sb("keyT", [P, GROUPS, 4], I32)
        relT = sb("relT", [P, GROUPS, 4])
        wT = sb("wT", [P, GROUPS, 4])
        idx = sb("idx", [P, 2, GPI * 4], I32)
        iotai = sb("iotai", [P, WIN], I32)
        iota = sb("iota", [P, WIN])
        S = sb("S", [P, SLOTS, 4, WIN])                
        red = sb("red", [P, 2])
        span = sb("span", [P, 2, 2])
        acc = sb("acc", [P, 2, F])
        grow = acc[0:1, :, :].rearrange("o u f -> o (u f)").rearrange("o (g k) -> o g k", k=2)
        scan = sb("scan", [1, 2, 64])
        half = sb("half", [1, 2, GPI // 2 * ROUNDS])
        tab = sb("tab", [1, ROUNDS, 4 + GPI], I32)
        tokS = hn
        hid = sb("hid", [P, 2, KH, BATCH])
        lg = sb("lg", [P, 2, EXP])
        pr = sb("pr", [P, 2, EXP])
        rank = sb("rank", [P, 2, EXP])
        comb = sb("comb", [P, 2, EXP])
        cmp = sb("cmp", [P, 2, EXP, EXP])
        cmp2 = sb("cmp2", [P, 2, EXP, EXP])
        lower = sb("lower", [P, EXP, EXP])
        col = sb("col", [P, 2])
        top = sb("top", [P, 2])
        combT = sb("combT", [EXP, 2, P])
        bank = [ctx.enter_context(nc.psum_tensor(f"bank{n}", [P, 512], FP32)) for n in range(8)]

        x_in = [sem(f"x_in{n}") for n in range(5)]
        small_in, b2_in, raw_in, grow_in = sem("small_in"), sem("b2_in"), sem("raw_in"), sem("grow_in")
        w_in = [sem(f"w_in{n}") for n in range(8)]
        exp_in = sem("exp_in")
        table_out = [sem("table_out0"), sem("table_out1")]
        rows_free = sem("rows_free")
        pool_chain = sem("pool_chain")
        ident_ok, small_zero, raw_zero, edges_ok, tabs_ok = (
            sem("ident_ok"), sem("small_zero"), sem("raw_zero"), sem("edges_ok"), sem("tabs_ok"))
        span_ok2 = sem("span_ok2")
        span_ok, span_out, tab_chain = sem("span_ok"), sem("span_out"), sem("tab_chain")
        iota_ok = sem("iota_ok")
        small_tr, small_ok = sem("small_tr"), sem("small_ok")
        res_zero = sem("res_zero")
        ln_chain, ln_pair = sem("ln_chain"), sem("ln_pair")
        w_high_ok, w_low_ok, hT_low_ok = sem("w_high_ok"), sem("w_low_ok"), sem("hT_low_ok")
        tr_done, hT_ok, gate_mm, gate_ok = sem("tr_done"), sem("hT_ok"), sem("gate_mm"), sem("gate_ok")
        mm_done, evac_act, evac_dve = sem("mm_done"), sem("evac_act"), sem("evac_dve")
        edge_tr, edge_ev = sem("edge_tr"), [sem("edge_act"), sem("edge_dve")]
        agg_zero, agg_zero_act, agg_zero_pool = sem("agg_zero"), sem("agg_zero_act"), sem("agg_zero_pool")
        turn_free = sem("turn_free")
        idx_ok = sem("idx_ok")
        gathered = [sem(f"gathered{r}") for r in range(GPI)]
        S_ok, seg_mm, added, shifted = sem("S_ok"), sem("seg_mm"), sem("added"), sem("shifted")
        relu_ok, agg_tr, tok_chain, tok_ok, tok_tr, xT_ok = (
            sem("relu_ok"), sem("agg_tr"), sem("tok_chain"), sem("tok_ok"), sem("tok_tr"), sem("xT_ok"))
        logit_mm, exp_ready, exp_ok, route_chain = (
            sem("logit_mm"), sem("exp_ready"), sem("exp_ok"), sem("route_chain"))
        comb_ok, top_ok = sem("comb_ok"), sem("top_ok")
        comb_tr, combT_ok, bias_mm, acc_done = sem("comb_tr"), sem("combT_ok"), sem("bias_mm"), sem("acc_done")
        h_mm, hid_ok, y_mm, y_added = sem("h_mm"), sem("hid_ok"), sem("y_mm"), sem("y_added")
        out_done, acc_free = sem("out_done"), sem("acc_free")
        bias_added = sem("bias_added")
        hold = sem("hold")

        def round_numbers(engine, i, registers):
            engine.load(registers, tab[0:1, bass.ds(i, 1), 0:len(registers)].rearrange("o r k -> o (r k)"))
            return (engine.snap(registers[0], min_val=0, max_val=NPAD // WIN),
                    engine.snap(registers[1], min_val=0, max_val=BATCHES),
                    engine.snap(registers[2], min_val=0, max_val=BATCHES))

        Y_BANK = [bank[n] for n in (4, 5, 0, 1, 0, 1, 4, 5)]
        Y_BEFORE = (None, None, None, None, 2, 3, 0, 1)

        block = ctx.enter_context(nc.Block())

        @block.sync
        def _(sp):
            def load_x(n, t0, t1):
                sp.dma_start(res[:, t0:t1, :], x[t0 * P:t1 * P, :].rearrange("(t p) f -> p t f", p=P)
                             ).then_inc(x_in[n], 16)
            sp.sem_inc(rows_free, 2)
            load_x(0, 0, 4)
            sp.wait_ge(small_zero, 1)
            sp.dma_start(small[0:R, :], ggate.rearrange("r f o -> r (f o)")).then_inc(small_in, 16)
            sp.dma_start(small[32:32 + EXP, :], router).then_inc(small_in, 16)
            sp.dma_start(small[64:64 + EXP * KH, 0:P], b1.rearrange("e (h p) -> (e h) p", p=P)).then_inc(small_in, 16)
            for n in range(8):
                for h in range(KH):
                    sp.dma_start(staged[:, n, h, :].rearrange("p (r o) -> p r o", r=2),
                                 gw[2 * n:2 * n + 2, h * P:(h + 1) * P, :].rearrange("r p o -> p r o")
                                 ).then_inc(w_in[n], 16)
            load_x(1, 4, STAGE_AT)
            sp.wait_ge(raw_zero, 1)
            for a, arr in enumerate((src, dst, etype, eweight)):
                out_dt = FP32 if a == 3 else I32
                flat = arr if a < 3 else arr.rearrange("e o -> (e o)")
                view = raw[:, a, :, :] if a == 3 else raw[:, a, :, :].bitcast(I32)
                sp.dma_start(view[:, 0, :], flat[0:P * GROUP].rearrange("(q e) -> q e", q=P)).then_inc(raw_in, 16)
                sp.dma_start(view[0:FULL - P, 1, :], flat[P * GROUP:FULL * GROUP].rearrange("(q e) -> q e", e=GROUP)
                             ).then_inc(raw_in, 16)
                sp.dma_start(view[FULL - P:FULL - P + 1, 1, 0:REST], flat[FULL * GROUP:E].rearrange("(q e) -> q e", q=1)
                             ).then_inc(raw_in, 16)
            sp.wait_ge(w_low_ok, R // 2)
            load_x(2, STAGE_AT, 34)
            load_x(3, 34, TILES - 1)
            sp.wait_ge(res_zero, 1)
            sp.dma_start(res[0:LAST_ROWS, TILES - 1, :], x[(TILES - 1) * P:N, :]).then_inc(x_in[4], 16)
            sp.dma_start(b2s[:, :], b2).then_inc(b2_in, 16)

            def write_half(slot, q2, node, count, rows_n=P):
                sp.wait_ge(evac_act, count)
                sp.wait_ge(evac_dve, count)
                span_ = R * F // 2
                dstv = table[bass.ds(node * R, rows_n * R), :].rearrange("(n r) f -> n (r f)", r=R)
                sp.dma_start(dstv[:, q2 * span_:(q2 + 1) * span_], rows[0:rows_n, slot, q2 * span_:(q2 + 1) * span_]
                             ).then_inc(table_out[slot], 16)

            def write_tiles(i0, i1):
                with sp.Fori(i0, i1) as i:
                    write_half(0, 0, i * (2 * P), i * 8 + 4)
                    write_half(0, 1, i * (2 * P), i * 8 + 6)
                    write_half(1, 0, i * (2 * P) + P, i * 8 + 8)
                    sp.wait_ge(table_out[0], i * 32 + 32)
                    sp.sem_inc(rows_free, 1)
                    write_half(1, 1, i * (2 * P) + P, i * 8 + 10)
                    sp.wait_ge(table_out[1], i * 32 + 32)
                    sp.sem_inc(rows_free, 1)

            write_tiles(0, TILES // 2)
            write_half(0, 0, (TILES - 1) * P, (TILES - 1) * 4 + 4, LAST_ROWS)
            write_half(0, 1, (TILES - 1) * P, (TILES - 1) * 4 + 6, LAST_ROWS)
            sp.wait_ge(mm_done, 8 * TILES + 16)
            for e in range(EXP):
                sp.wait_ge(gathered[e], 4 * 16)
                for w_t, w_s in ((w1, w1s), (w2, w2s)):
                    sp.dma_start(w_s[:, e, :, :], w_t[e, :, :].rearrange("(h p) o -> p h o", p=P)).then_inc(exp_in, 16)

            sent = sp.alloc_register("sent")
            sp.reg_mov(sent, 0)
            row = [sp.alloc_register(f"row{k}") for k in range(4)]
            sp.sem_inc(acc_free, 1)
            sp.wait_ge(tabs_ok, 1)
            with sp.Fori(0, ROUNDS) as i:
                _, lo, hi = round_numbers(sp, i, row)
                first = sp.snap((lo < 1) * 1 + lo, min_val=0, max_val=BATCHES)
                with sp.If(first < hi):
                    with sp.Fori(first, hi):
                        b = sp.snap(sent, min_val=0, max_val=BATCHES - 2)
                        sp.wait_ge(acc_done, b + 2)
                        sp.dma_start(out[bass.ds(b * BATCH, BATCH), :].rearrange("(u p) f -> p u f", p=P),
                                     acc[:, :, :]).then_inc(out_done, 16)
                        sp.wait_ge(out_done, b * 16 + 16)
                        sp.sem_inc(acc_free, 1)
                        sp.reg_add(sent, sent, 1)
            sp.wait_ge(acc_done, BATCHES + 1)
            left = N - (BATCHES - 1) * BATCH
            for u in range(2):
                n0 = (BATCHES - 1) * BATCH + u * P
                n1 = min(n0 + P, N)
                if n1 > n0:
                    sp.dma_start(out[n0:n1, :], acc[0:n1 - n0, u, :]).then_inc(out_done, 16)
            sp.wait_ge(out_done, 16 * (BATCHES - 1) + 16 * (-(-left // P)))

        @block.gpsimd
        def _(pool):
            chain = Chain(pool, pool_chain)
            chain(pool.memset(small[:, :], 0.0))
            pool.sem_inc(small_zero, 1)
            chain(pool.memset(ident[:, :], 0.0))
            pool.affine_select(out=ident[:, :], in_=ident[:, :], compare_op=ALU.not_equal, fill=1.0, base=0,
                               pattern=[[-1, P]], channel_multiplier=1).then_inc(ident_ok, 1)
            pool.memset(raw[:, 0, 1, :].bitcast(I32), 0)
            pool.memset(raw[:, 1, 1, :].bitcast(I32), N - 1)
            pool.memset(raw[:, 2, 1, :].bitcast(I32), 0)
            pool.memset(raw[:, 3, 1, :], 0.0).then_inc(raw_zero, 1)
            pool.iota(iotai[:, :], pattern=[[1, WIN]], base=0, channel_multiplier=0).then_inc(iota_ok, 1)
            pool.wait_ge(iota_ok, 1)
            pool.tensor_copy(iota[:, :], iotai[:, :]).then_inc(iota_ok, 1)
            chain(pool.memset(lower[:, :, :], 1.0))
            chain(pool.affine_select(out=lower[:, :, :], in_=lower[:, :, :], compare_op=ALU.is_gt, fill=0.0, base=0,
                                     pattern=[[1, EXP], [-1, EXP]], channel_multiplier=0))
            pool.wait_ge(span_ok, 1)
            chain(pool.tensor_copy(raw[:, 1, :, :], raw[:, 1, :, :].bitcast(I32)))
            for b in range(2):
                chain(pool.tensor_scalar(raw[:, 1, b, :], raw[:, 1, b, :], span[:, b, 0:1], None, ALU.subtract))
            chain(pool.tensor_scalar(raw[:, 0, :, :], raw[:, 0, :, :].bitcast(I32), float(R), None, ALU.mult))
            chain(pool.tensor_copy(raw[:, 2, :, :], raw[:, 2, :, :].bitcast(I32)))
            pool.tensor_tensor(raw[:, 0, :, :], raw[:, 0, :, :], raw[:, 2, :, :], ALU.add
                               ).then_inc(edges_ok, 1)
            pool.dma_start(group_dram.rearrange("(b q) k -> q b k", q=P), span[:, :, :]).then_inc(span_out, 16)
            pool.wait_ge(span_out, 16)
            pool.dma_start(grow[:, :, :], group_dram.rearrange("(o g) k -> o g k", o=1)).then_inc(grow_in, 16)

            pool.wait_ge(edge_ev[0], 3)
            pool.wait_ge(edge_ev[1], 3)
            pool.memset(agg[:, ZERO[2]:ZERO[3]], 0.0).then_inc(agg_zero_pool, 1)
            pool.wait_ge(table_out[0], 32 * (TILES // 2 + 1))
            pool.wait_ge(table_out[1], 32 * (TILES // 2))
            pool.sem_inc(hold, 1)
            passes = pool.alloc_register("passes")
            pool.reg_mov(passes, 0)
            with pool.Fori(0, ROUNDS // 2) as i:
                for h in range(2):
                    extra = pool.value_load(tab[0:1, bass.ds(i * 2 + h, 1), 0:1].rearrange("o r k -> o (r k)"),
                                            min_val=0, max_val=NPAD // WIN)
                    p = pool.snap(passes, min_val=0, max_val=1 << 20)
                    pool.wait_ge(seg_mm, p * GPI + 1)
                    pool.sem_inc(hold, 1)
                    pool.tensor_copy(idx[:, h, :], keyT[:, bass.ds(i * (2 * GPI) + h * GPI, GPI), :].rearrange("p g j -> p (g j)")
                                     ).then_inc(idx_ok, 1)
                    pool.wait_ge(idx_ok, i * 2 + (h + 1))
                    for r in range(GPI):
                        pool.wait_ge(seg_mm, p * GPI + (r + 1))
                        pool.sem_inc(turn_free, 1)
                        for j in range(4):
                            pool.indirect_dma_start(
                                out=ring[:, r * 4 + j, :], out_offset=None, in_=table[:, :],
                                in_offset=bass.IndirectOffsetOnAxis(ap=idx[:, h, r * 4 + j:r * 4 + j + 1], axis=0),
                            ).then_inc(gathered[r], 16)
                    pool.reg_add(passes, passes, extra + 1)

        @block.scalar
        def _(act):
            act.sem_inc(evac_act, 2)
            act.sem_inc(hT_ok, 2)
            act.sem_inc(gate_ok, 1)
            act.wait_ge(small_tr, 1)
            act.activation(smallT[:, :, :], bank[7][:, 0:KH * P].rearrange("p (h q) -> p h q", h=KH), ACT.Copy
                           ).then_inc(small_ok, 1)
            act.wait_ge(small_ok, 1)
            act.activation(gate_high[:, :, :], smallT[:, :, 0:R], ACT.Copy).then_inc(small_ok, 1)

            def copy_hT(u, t):
                act.wait_ge(tr_done, t + 3)
                act.wait_ge(mm_done, t * 8 + 8)
                act.activation(hT[:, u, :, :], bank[4 + u][:, 0:KH * P].rearrange("p (h q) -> p h q", h=KH), ACT.Copy
                               ).then_inc(hT_ok, 1)

            def gates_and_rows(u, t):
                act.wait_ge(gate_mm, t + 1)
                act.wait_ge(rows_free, t + 1)
                act.activation(gate[:, u, :], bank[6][:, 0:R], ACT.Sigmoid).then_inc(gate_ok, 1)
                act.wait_ge(gate_ok, t + 2)
                for k in range(4):
                    q = 2 * k
                    act.wait_ge(mm_done, t * 8 + (q + 17))
                    for r in range(2):
                        ins = act.activation(rows[:, u, (2 * q + r) * F:(2 * q + r + 1) * F],
                                             bank[q % 4][:, r * F:(r + 1) * F], ACT.Copy,
                                             scale=gate[:, u, 2 * q + r:2 * q + r + 1])
                    ins.then_inc(evac_act, 1)

            copy_hT(0, 0)
            for q in range(R // 2):
                act.wait_ge(w_in[q], 32)
                act.activation(w_high[:, q, :, :], staged[:, q, :, :], ACT.Copy).then_inc(w_high_ok, 1)

            def part1(i0, i1):
                with act.Fori(i0, i1) as i:
                    copy_hT(1, i * 2 + 1)
                    gates_and_rows(0, i * 2)
                    copy_hT(0, i * 2 + 2)
                    gates_and_rows(1, i * 2 + 1)

            part1(0, THIRD[1])
            for n, dst_ in ((0, keyT), (2, relT), (4, wT)):
                act.wait_ge(edge_tr, n + 1)
                act.activation(dst_[:, 0:P, :].rearrange("p g j -> p j g"),
                               bank[7][:, :].rearrange("p (j g) -> p j g", j=4), ACT.Copy).then_inc(edge_ev[0], 1)
            part1(THIRD[1], TILES // 2)
            gates_and_rows(0, TILES - 1)

            act.wait_ge(mm_done, 8 * TILES + 16)
            act.wait_ge(agg_zero_pool, 1)
            act.activation(agg[:, ZERO[0]:ZERO[1]], agg[:, ZERO[2]:ZERO[3]], ACT.Copy).then_inc(agg_zero_act, 1)
            act.sem_inc(hid_ok, 2)
            act.wait_ge(tabs_ok, 1)
            done = act.alloc_register("batches")
            act.reg_mov(done, 0)
            row = [act.alloc_register(f"row{k}") for k in range(4)]
            mixed = act.alloc_register("mixed")
            act.reg_mov(mixed, 0)

            def experts(b, tiles=2):
                for e in range(EXP):
                    act.wait_ge(h_mm, b * EXP + (e + 1))
                    act.wait_ge(y_mm, b * EXP + (e + 1))
                    for h in range(KH):
                        ins = act.activation(hid[:, e % 2, h, 0:tiles * P],
                                             bank[2 + e % 2][:, h * BATCH:h * BATCH + tiles * P],
                                             ACT.Gelu, bias=smallT[:, 0, 64 + e * KH + h:65 + e * KH + h])
                    ins.then_inc(hid_ok, 1)

            with act.Fori(0, ROUNDS) as i:
                _, lo, hi = round_numbers(act, i, row)
                with act.If(lo < hi):
                    with act.Fori(lo, hi):
                        f = act.snap(done, min_val=0, max_val=BATCHES - 1)
                        with act.If(f > 0):
                            experts(act.snap(mixed, min_val=0, max_val=BATCHES - 2))
                            act.reg_add(mixed, mixed, 1)
                        act.wait_ge(tok_tr, f + 1)
                        act.activation(xT[:, :, :], bank[6][:, :].rearrange("p (h n) -> p h n", h=KH), ACT.Copy
                                       ).then_inc(xT_ok, 1)
                        act.wait_ge(exp_ready, f + 1)
                        act.activation(pr[:, :, :], lg[:, :, :], ACT.Exp).then_inc(exp_ok, 1)
                        act.reg_add(done, done, 1)
            experts(BATCHES - 1, LAST_TILES)

        @block.vector
        def _(dve):
            dve.sem_inc(evac_dve, 2)
            dve.sem_inc(hT_low_ok, 2)

            def rstd_of(chain, width):
                v, y, t = var[:, 0:width], rstd[:, 0:width], tmp[:, 0:width]
                chain(dve.tensor_scalar(v, mv[:, 0:width, 1], EPS, None, ALU.add))
                chain(dve.tensor_scalar(ybits[:, 0:width], v.bitcast(I32), 1, None, ALU.arith_shift_right))
                chain(dve.tensor_scalar(y.bitcast(I32), ybits[:, 0:width], -1.0, RSQRT_MAGIC, ALU.mult, ALU.add))
                for _ in range(3):
                    chain(dve.tensor_tensor(t, y, y, ALU.mult))
                    chain(dve.tensor_tensor(t, t, v, ALU.mult))
                    chain(dve.tensor_scalar(t, t, -0.5, 1.5, ALU.mult, ALU.add))
                    chain(dve.tensor_tensor(y, y, t, ALU.mult))

            def stats(chain, tile):
                for u in range(2):
                    dve.sem_inc(hold, 1)
                    chain(dve.bn_stats(stat[:, u, :], tile(u)))
                for u in range(2):
                    dve.sem_inc(hold, 1)
                    chain(dve.bn_aggr(mv[:, u, :], stat[:, u, :]))
                rstd_of(chain, 2)

            def norm_pair(chain, t):
                for u in range(2):
                    dve.wait_ge(tr_done, t + (1 + u))
                    dve.sem_inc(hold, 1)
                    dve.tensor_scalar(hn[:, u, :], res[:, bass.ds(t + u, 1), :].rearrange("p o f -> p (o f)"),
                                      mv[:, u, 0:1], rstd[:, u:u + 1], ALU.subtract, ALU.mult).then_inc(ln_pair, 1)

            def rows_of(t):
                return lambda u: res[:, bass.ds(t + u, 1), :].rearrange("p o f -> p (o f)")

            def evacuate(u, t, k):
                q = 2 * k + 1
                dve.wait_ge(mm_done, t * 8 + (q + 17))
                dve.tensor_tensor(rows[:, u, 2 * q * F:(2 * q + 2) * F].rearrange("p (r f) -> p r f", r=2),
                                  bank[q % 4][:, :].rearrange("p (r f) -> p r f", r=2),
                                  gate[:, u, 2 * q:2 * q + 2].unsqueeze(2).to_broadcast([P, 2, F]), ALU.mult
                                  ).then_inc(evac_dve, 1)

            def low_hT(u, t):
                dve.wait_ge(hT_ok, t + 3)
                dve.tensor_tensor(hT_low[:, u, :, :], bank[4 + u][:, 0:KH * P].rearrange("p (h q) -> p h q", h=KH),
                                  hT[:, u, :, :].bitcast(FP32), ALU.subtract).then_inc(hT_low_ok, 1)

            LINKS = 4 + 3 + 12
            dve.wait_ge(x_in[0], 16)
            first = Chain(dve, ln_chain)
            stats(first, rows_of(0))
            norm_pair(None, 0)
            assert first.n == LINKS
            dve.wait_ge(small_ok, 2)
            dve.tensor_tensor(gate_low[:, :, :], smallT[:, :, 0:R], gate_high[:, :, :].bitcast(FP32), ALU.subtract
                              ).then_inc(small_ok, 1)
            low_hT(0, 0)
            for q in range(R // 2):
                dve.wait_ge(w_high_ok, q + 1)
                dve.tensor_tensor(w_low[:, q, :, :], staged[:, q, :, :], w_high[:, q, :, :].bitcast(FP32), ALU.subtract
                                  ).then_inc(w_low_ok, 1)
            dve.wait_ge(w_low_ok, R // 2)
            dve.memset(res[:, TILES - 1:2 * BATCHES, :], 0.0).then_inc(res_zero, 1)

            def part1(i0, i1):
                with dve.Fori(i0, i1) as i:
                    for u in range(2):
                        t = i * 2 + u
                        low_hT(1 - u, t + 1)
                        dve.wait_ge(gate_ok, t + 2)
                        dve.wait_ge(rows_free, t + 1)
                        for k in range(4):
                            evacuate(u, t, k)
                            if u == 0 and k == 0:
                                c = Chain(dve, ln_chain, (i + 1) * LINKS)
                                dve.wait_ge(ln_pair, i * 2 + 2)
                                stats(c, rows_of(i * 2 + 2))
                                assert c.n == LINKS
                            if u == 0 and k == 1:
                                norm_pair(None, i * 2 + 2)
                    dve.wait_ge(x_in[1], 16)

            part1(0, THIRD[0])
            dve.wait_ge(raw_in, 12 * 16)
            dve.tensor_reduce(span[:, :, 0], raw[:, 1, :, :].bitcast(I32), AX.X, ALU.min).then_inc(span_ok2, 1)
            dve.tensor_reduce(red[:, :], raw[:, 1, :, :].bitcast(I32), AX.X, ALU.max).then_inc(span_ok2, 1)
            dve.wait_ge(span_ok2, 2)
            dve.tensor_tensor(span[:, :, 1], red[:, :], span[:, :, 0], ALU.subtract).then_inc(span_ok, 1)
            dve.wait_ge(x_in[2], 16)
            part1(THIRD[0], THIRD[1])
            chain = Chain(dve, tab_chain)
            dve.wait_ge(grow_in, 16)
            lows, spans = grow[0:1, 0:GROUPS, 0], grow[0:1, 0:GROUPS, 1]
            chain(dve.memset(tab[0:1, :, :], 0))
            chain(dve.tensor_copy(tab[0:1, :, 4:4 + GPI], lows.rearrange("o (r g) -> o r g", g=GPI)))

            def over_groups(v, k, op):
                a = v.rearrange("o (r g) -> o r g", g=GPI)
                n = GPI // 2
                dst_ = half[0:1, k, :].rearrange("o (r g) -> o r g", g=n)
                chain(dve.tensor_tensor(dst_, a[:, :, 0:n], a[:, :, n:2 * n], op))
                while n > 1:
                    n //= 2
                    chain(dve.tensor_tensor(dst_[:, :, 0:n], dst_[:, :, 0:n], dst_[:, :, n:2 * n], op))
                return dst_[:, :, 0]
            widest = over_groups(spans, 0, ALU.max)
            chain(dve.tensor_scalar(tab[0:1, :, 0], widest, 1.0 / WIN, 0.5 / WIN - 0.5, ALU.mult, ALU.add))
            lowest = over_groups(lows, 1, ALU.min)
            chain(dve.memset(scan[0:1, :, :], float(NPAD)))
            chain(dve.tensor_copy(scan[0:1, 0, 0:ROUNDS - 1], lowest[:, 1:ROUNDS]))
            step, k = 1, 0
            while step < ROUNDS:
                chain(dve.tensor_tensor(scan[0:1, 1 - k, 0:ROUNDS], scan[0:1, k, 0:ROUNDS],
                                         scan[0:1, k, step:step + ROUNDS], ALU.min))
                step, k = 2 * step, 1 - k
            for at, count, c in ((0, ROUNDS, 2), (1, ROUNDS - 1, 1)):
                chain(dve.tensor_scalar(tab[0:1, at:ROUNDS, c], scan[0:1, k, 0:count], 1.0 / BATCH,
                                        0.5 / BATCH - 0.5, ALU.mult, ALU.add))
            dve.sem_inc(tabs_ok, 1)
            for n, dst_ in ((1, keyT), (3, relT), (5, wT)):
                dve.wait_ge(edge_tr, n + 1)
                dve.tensor_copy(dst_[:, P:GROUPS, :].rearrange("p g j -> p j g"),
                                bank[6][:, :].rearrange("p (j g) -> p j g", j=4)[:, :, 0:GROUPS - P]).then_inc(edge_ev[1], 1)
            dve.wait_ge(x_in[3], 16)
            dve.wait_ge(x_in[4], 16)
            part1(THIRD[1], TILES // 2)
            dve.wait_ge(gate_ok, TILES + 1)
            dve.wait_ge(rows_free, TILES)
            for k in range(4):
                evacuate(0, TILES - 1, k)

            dve.wait_ge(mm_done, 8 * TILES + 16)
            dve.memset(agg[:, 0:ZERO[0]], 0.0).then_inc(agg_zero, 1)
            dve.memset(agg[:, ZERO[3]:KH * AGGW], 0.0).then_inc(agg_zero, 1)
            dve.sem_inc(added, 2)
            dve.sem_inc(shifted, 1)
            dve.sem_inc(y_added, 2)
            dve.sem_inc(acc_done, 1)
            dve.sem_inc(bias_added, 1)
            dve.wait_ge(tabs_ok, 1)
            dve.wait_ge(iota_ok, 2)
            dve.wait_ge(edge_ev[0], 3)
            dve.wait_ge(edge_ev[1], 3)
            dve.wait_ge(agg_zero, 2)
            dve.wait_ge(agg_zero_act, 1)
            passes = dve.alloc_register("passes")
            done = dve.alloc_register("batches")
            base = dve.alloc_register("base")
            following = dve.alloc_register("following")
            row = [dve.alloc_register(f"row{k}") for k in range(4 + GPI)]
            dve.reg_mov(passes, 0)
            dve.reg_mov(done, 0)
            mixed = dve.alloc_register("mixed")
            dve.reg_mov(mixed, 0)

            def combT_copy(b):
                dve.wait_ge(comb_tr, b + 2)
                dve.tensor_copy(combT[:, :, :], bank[7][0:EXP, 0:2 * P].rearrange("e (u p) -> e u p", u=2)
                                ).then_inc(combT_ok, 1)

            def experts(b, tiles=2):
                dve.wait_ge(acc_free, b + 1)
                for e in range(EXP):
                    dve.wait_ge(y_mm, b * EXP + (e + 3))
                    for u in range(tiles):
                        dve.wait_ge(y_added, b * (2 * EXP) + (tiles * (e - 1) + u + 3))
                        if e == 0:
                            dve.sem_inc(hold, 1)
                        before = rows_of(b * 2)(u) if e == 0 else acc[:, u, :]
                        dve.scalar_tensor_tensor(acc[:, u, :], Y_BANK[e][:, u * F:(u + 1) * F],
                                                 comb[:, u, e:e + 1], before, ALU.mult, ALU.add
                                                 ).then_inc(y_added, 1)
                    if e == 1:
                        combT_copy(b)
                    if e == BIAS_AT:
                        dve.wait_ge(bias_mm, b + 1)
                        dve.wait_ge(y_added, b * (2 * EXP) + (tiles * (e + 1) + 2))
                        dve.tensor_tensor(acc[:, 0:tiles, :], acc[:, 0:tiles, :],
                                          bank[7][:, 0:tiles * F].rearrange("p (u f) -> p u f", u=tiles), ALU.add).then_inc(bias_added, 1)
                        dve.wait_ge(bias_added, b + 2)
                dve.wait_ge(y_added, b * (2 * EXP) + (tiles * EXP + 2))
                dve.sem_inc(acc_done, 1)

            TOK_LINKS = 1 + LINKS
            ROUTE_LINKS = 2 + 6 + 5

            def tokens(f):
                c = Chain(dve, tok_chain, f * TOK_LINKS)
                pair = res[:, bass.ds(f * 2, 2), :]
                dve.wait_ge(agg_tr, f + 2)
                chain_in = dve.tensor_tensor(pair, bank[6][:, :].rearrange("p (u f) -> p u f", u=2), pair, ALU.add)
                c(chain_in)
                stats(c, rows_of(f * 2))
                for u in range(2):
                    dve.tensor_scalar(tokS[:, u, :], rows_of(f * 2)(u), mv[:, u, 0:1], rstd[:, u:u + 1],
                                      ALU.subtract, ALU.mult).then_inc(tok_ok, 1)
                assert c.n == TOK_LINKS
                dve.wait_ge(tok_ok, f * 3 + 2)
                dve.tensor_tensor(pair, pair, tokS[:, :, :], ALU.add).then_inc(tok_ok, 1)

            def shift_logits(f):
                dve.wait_ge(logit_mm, f + 1)
                L = bank[7][:, 0:2 * EXP].rearrange("p (u e) -> p u e", u=2)
                dve.tensor_reduce(top[:, :], L, AX.X, ALU.max).then_inc(top_ok, 1)
                dve.wait_ge(top_ok, f + 1)
                dve.tensor_tensor(lg[:, :, :], L, top[:, :].unsqueeze(2).to_broadcast([P, 2, EXP]), ALU.subtract
                                  ).then_inc(exp_ready, 1)

            def route(f):
                c = Chain(dve, route_chain, f * ROUTE_LINKS)
                dve.wait_ge(exp_ok, f + 1)
                c(dve.tensor_reduce(col[:, :], pr[:, :, :], AX.X, ALU.add))
                c(dve.reciprocal(col[:, :], col[:, :]))
                c(dve.tensor_tensor(pr[:, :, :], pr[:, :, :], col[:, :].unsqueeze(2).to_broadcast([P, 2, EXP]), ALU.mult))
                pj = pr[:, :, :].unsqueeze(2).to_broadcast([P, 2, EXP, EXP])
                pe_ = pr[:, :, :].unsqueeze(3).to_broadcast([P, 2, EXP, EXP])
                low_ = lower[:, :, :].unsqueeze(1).to_broadcast([P, 2, EXP, EXP])
                c(dve.tensor_tensor(cmp[:, :, :, :], pj, pe_, ALU.is_gt))
                c(dve.tensor_tensor(cmp2[:, :, :, :], pj, pe_, ALU.is_equal))
                c(dve.tensor_tensor(cmp2[:, :, :, :], cmp2[:, :, :, :], low_, ALU.mult))
                c(dve.tensor_tensor(cmp[:, :, :, :], cmp[:, :, :, :], cmp2[:, :, :, :], ALU.add))
                c(dve.tensor_reduce(rank[:, :, :], cmp[:, :, :, :], AX.X, ALU.add))
                c(dve.scalar_tensor_tensor(pr[:, :, :], rank[:, :, :], 1.5, pr[:, :, :], ALU.is_lt, ALU.mult))
                c(dve.tensor_reduce(col[:, :], pr[:, :, :], AX.X, ALU.add))
                c(dve.tensor_scalar(col[:, :], col[:, :], 1e-12, None, ALU.max))
                c(dve.reciprocal(col[:, :], col[:, :]))
                dve.wait_ge(y_added, f * (2 * EXP) + 2)
                dve.wait_ge(comb_tr, f + 1)
                c(dve.tensor_tensor(comb[:, :, :], pr[:, :, :], col[:, :].unsqueeze(2).to_broadcast([P, 2, EXP]), ALU.mult))
                assert c.n == ROUTE_LINKS, c.n
                dve.sem_inc(comb_ok, 1)

            def weights_by_target(slot, g, seg_count):
                dve.wait_ge(seg_mm, seg_count)
                dve.sem_inc(hold, 1)
                for j in range(4):
                    ins = dve.tensor_scalar(S[:, slot % SLOTS, j, :], iota[:, :],
                                            relT[:, bass.ds(g, 1), j:j + 1].rearrange("p o k -> p (o k)"),
                                            wT[:, bass.ds(g, 1), j:j + 1].rearrange("p o k -> p (o k)"),
                                            ALU.is_equal, ALU.mult)
                ins.then_inc(S_ok, 1)

            for r in range(LEAD):
                weights_by_target(r, r, GPI)
            with dve.Fori(0, ROUNDS) as i:
                extra, lo, hi = round_numbers(dve, i, row)
                with dve.Fori(0, extra + 1) as w:
                    p = dve.snap(passes, min_val=0, max_val=1 << 20)
                    for r in range(GPI):
                        low_ = dve.snap(row[4 + r], min_val=0, max_val=NPAD - 1)
                        dve.reg_alu(base, low_ + w * WIN, NPAD, ALU.min)
                        to = dve.snap(base, min_val=0, max_val=NPAD)
                        dve.wait_ge(seg_mm, p * GPI + (r + GPI + 1))
                        dve.wait_ge(added, p * GPI + (r + 2))
                        window = aggv[:, :, bass.ds(to, WIN)]
                        dve.tensor_tensor(window, window,
                                          bank[r % 2][:, 0:KH * WIN].rearrange("p (h n) -> p h n", h=KH), ALU.add
                                          ).then_inc(added, 1)
                        if r + LEAD < GPI:
                            weights_by_target(r + LEAD, i * GPI + (r + LEAD), p * GPI + (r + LEAD + 1 + GPI - SLOTS))
                    dve.wait_ge(S_ok, p * GPI + GPI)
                    dve.sem_inc(hold, 1)
                    moved = relT[:, bass.ds(i * GPI, GPI), :]
                    dve.tensor_scalar(moved, moved, float(WIN), None, ALU.subtract).then_inc(shifted, 1)
                    dve.wait_ge(shifted, p + 2)
                    dve.reg_alu(following, w + 1, extra + 1, ALU.is_ge)
                    dve.reg_add(following, following, i)
                    dve.reg_alu(following, following, ROUNDS - 1, ALU.min)
                    nxt = dve.snap(following, min_val=0, max_val=ROUNDS - 1)
                    for r in range(LEAD):
                        weights_by_target(r, nxt * GPI + r, p * GPI + 2 * GPI)
                    dve.reg_add(passes, passes, 1)
                with dve.If(lo < hi):
                    with dve.Fori(lo, hi):
                        f = dve.snap(done, min_val=0, max_val=BATCHES - 1)
                        dve.wait_ge(added, dve.snap(passes, min_val=0, max_val=1 << 20) * GPI + 2)
                        dve.wait_ge(agg_tr, f + 1)
                        dve.sem_inc(hold, 1)
                        dve.tensor_scalar(aggS[:, :, :], aggv[:, :, bass.ds(f * BATCH, BATCH)], 0.0, None, ALU.max
                                          ).then_inc(relu_ok, 1)
                        with dve.If(f > 0):
                            route(dve.snap(mixed, min_val=0, max_val=BATCHES - 2))
                        tokens(f)
                        with dve.If(f > 0):
                            experts(dve.snap(mixed, min_val=0, max_val=BATCHES - 2))
                            dve.reg_add(mixed, mixed, 1)
                        shift_logits(f)
                        dve.reg_add(done, done, 1)
            route(BATCHES - 1)
            experts(BATCHES - 1, LAST_TILES)

        @block.tensor
        def _(pe):
            pe.wait_ge(ident_ok, 1)
            pe.wait_ge(small_in, 48)
            for h in range(KH):
                ins = pe.transpose(bank[7][:, h * P:(h + 1) * P], small[:, h * P:(h + 1) * P], ident[:, :])
            ins.then_inc(small_tr, 1)
            pe.sem_inc(tr_done, 2)
            pe.sem_inc(mm_done, 16)

            def transposes(u, t):
                pe.wait_ge(ln_pair, t + 1)
                pe.wait_ge(hT_low_ok, t + 1)
                for h in range(KH):
                    ins = pe.transpose(bank[4 + u][:, h * P:(h + 1) * P], hn[:, u, h * P:(h + 1) * P], ident[:, :])
                ins.then_inc(tr_done, 1)

            def exact(dst_, pairs):
                for n, (left, right) in enumerate(pairs):
                    ins = pe.matmul(dst_, left, right, start=n == 0, stop=n == len(pairs) - 1)
                return ins

            def messages(u, t):
                pe.wait_ge(hT_low_ok, t + 3)
                pe.wait_ge(gate_ok, t + 1)
                high, low = hT[:, u, :, :], hT_low[:, u, :, :]
                ins = exact(bank[6][:, 0:R], [pair for h in range(KH) for pair in (
                    (high[:, h, :], gate_high[:, h, :]), (high[:, h, :], gate_low[:, h, :]),
                    (low[:, h, :], gate_high[:, h, :]))])
                ins.then_inc(gate_mm, 1)
                for q in range(8):
                    pe.wait_ge(w_low_ok, q + 1)
                    pe.wait_ge((evac_act, evac_dve)[q % 2], t * 4 + (q // 2 + 1))
                    ins = exact(bank[q % 4][:, :], [pair for h in range(KH) for pair in (
                        (high[:, h, :], w_high[:, q, h, :]), (high[:, h, :], w_low[:, q, h, :]),
                        (low[:, h, :], w_high[:, q, h, :]))])
                    ins.then_inc(mm_done, 1)

            transposes(0, 0)
            pe.wait_ge(small_ok, 3)

            def part1(i0, i1):
                with pe.Fori(i0, i1) as i:
                    transposes(1, i * 2 + 1)
                    messages(0, i * 2)
                    transposes(0, i * 2 + 2)
                    messages(1, i * 2 + 1)

            part1(0, THIRD[1])
            pe.wait_ge(edges_ok, 1)
            pe.wait_ge(gate_ok, 2 * THIRD[1] + 1)
            for n, a in enumerate((0, 0, 1, 1, 3, 3)):
                if n >= 2:
                    pe.wait_ge(edge_ev[n % 2], n // 2)
                for j in range(4):
                    ins = pe.transpose(bank[7 if n % 2 == 0 else 6][:, j * P:(j + 1) * P],
                                       raw[:, a, n % 2, j * P:(j + 1) * P], ident[:, :])
                ins.then_inc(edge_tr, 1)
            pe.wait_ge(edge_ev[0], 3)
            pe.wait_ge(edge_ev[1], 3)
            part1(THIRD[1], TILES // 2)
            messages(0, TILES - 1)

            pe.wait_ge(evac_act, 4 * TILES + 2)
            pe.wait_ge(evac_dve, 4 * TILES + 2)
            pe.wait_ge(b2_in, 16)
            pe.wait_ge(tabs_ok, 1)
            pe.sem_inc(seg_mm, GPI)
            pe.sem_inc(agg_tr, 1)
            pe.sem_inc(y_mm, 2)
            pe.sem_inc(comb_tr, 1)
            passes = pe.alloc_register("passes")
            done = pe.alloc_register("batches")
            pe.reg_mov(passes, 0)
            pe.reg_mov(done, 0)
            row = [pe.alloc_register(f"row{k}") for k in range(4)]
            mixed = pe.alloc_register("mixed")
            pe.reg_mov(mixed, 0)

            def combine_T(b):
                pe.wait_ge(comb_ok, b + 1)
                for u in range(2):
                    ins = pe.transpose(bank[7][0:EXP, u * P:(u + 1) * P], comb[:, u, :], ident[:, :])
                ins.then_inc(comb_tr, 1)

            def hidden(b, e, tiles=2):
                pe.wait_ge(hid_ok, b * EXP + (e + 1))
                for m in range(KH):
                    for h in range(KH):
                        ins = pe.matmul(bank[2 + e % 2][:, m * BATCH:m * BATCH + tiles * P],
                                        w1s[:, e, h, m * P:(m + 1) * P], xT[:, h, 0:tiles * P], start=h == 0, stop=h == KH - 1)
                ins.then_inc(h_mm, 1)

            def project(b, e, tiles=2):
                pe.wait_ge(hid_ok, b * EXP + (e + 3))
                if Y_BEFORE[e] is not None:
                    pe.wait_ge(y_added, b * (2 * EXP) + (tiles * (Y_BEFORE[e] + 1) + 2))
                for u in range(tiles):
                    for m in range(KH):
                        ins = pe.matmul(Y_BANK[e][:, u * F:(u + 1) * F], hid[:, e % 2, m, u * P:(u + 1) * P],
                                        w2s[:, e, m, :], start=m == 0, stop=m == KH - 1)
                ins.then_inc(y_mm, 1)

            def first_experts(b, tiles=2):
                pe.wait_ge(exp_in, 2 * EXP * 16)
                hidden(b, 0, tiles)
                hidden(b, 1, tiles)
                project(b, 0, tiles)
                hidden(b, 2, tiles)

            def experts(b, tiles=2, next_tokens=None):
                for e in range(1, EXP):
                    project(b, e, tiles)
                    if e + 2 < EXP:
                        hidden(b, e + 2, tiles)
                    if e == 2:
                        combine_T(b)
                    if e == 3:
                        pe.wait_ge(combT_ok, b + 1)
                        for u in range(2):
                            ins = pe.matmul(bank[7][:, u * F:(u + 1) * F], combT[:, u, :], b2s[:, :], start=True, stop=True)
                        ins.then_inc(bias_mm, 1)
                    if e == EXP - 3 and next_tokens is not None:
                        next_tokens()
                pe.wait_ge(y_added, b * (2 * EXP) + (tiles * (EXP - 2) + 2))

            with pe.Fori(0, ROUNDS) as i:
                extra, lo, hi = round_numbers(pe, i, row)
                with pe.Fori(0, extra + 1):
                    p = pe.snap(passes, min_val=0, max_val=1 << 20)
                    for r in range(GPI):
                        pe.wait_ge(gathered[r], i * 64 + 64)
                        pe.wait_ge(S_ok, p * GPI + (r + 1))
                        pe.wait_ge(added, p * GPI + (r + 1))
                        for h in range(KH):
                            for j in range(4):
                                ins = pe.matmul(bank[r % 2][:, h * WIN:(h + 1) * WIN], ring[:, r * 4 + j, h * P:(h + 1) * P],
                                                S[:, r % SLOTS, j, :], start=j == 0, stop=j == 3)
                        ins.then_inc(seg_mm, 1)
                    pe.reg_add(passes, passes, 1)
                with pe.If(lo < hi):
                    with pe.Fori(lo, hi):
                        f = pe.snap(done, min_val=0, max_val=BATCHES - 1)
                        with pe.If(f > 0):
                            first_experts(pe.snap(mixed, min_val=0, max_val=BATCHES - 2))
                        pe.wait_ge(relu_ok, f + 1)
                        for u in range(2):
                            for h in range(KH):
                                ins = pe.transpose(bank[6][:, u * F + h * P:u * F + (h + 1) * P],
                                                   aggS[:, h, u * P:(u + 1) * P], ident[:, :])
                        ins.then_inc(agg_tr, 1)
                        def transpose_tokens():
                            pe.wait_ge(tok_ok, f * 3 + 3)
                            for h in range(KH):
                                for u in range(2):
                                    ins = pe.transpose(bank[6][:, h * BATCH + u * P:h * BATCH + (u + 1) * P],
                                                       tokS[:, u, h * P:(h + 1) * P], ident[:, :])
                            ins.then_inc(tok_tr, 1)
                        with pe.If(f > 0):
                            experts(pe.snap(mixed, min_val=0, max_val=BATCHES - 2), 2, transpose_tokens)
                            pe.reg_add(mixed, mixed, 1)
                        with pe.If(f < 1):
                            transpose_tokens()
                        pe.wait_ge(xT_ok, f + 1)
                        pe.wait_ge(bias_added, f + 1)
                        for u in range(2):
                            for h in range(KH):
                                ins = pe.matmul(bank[7][:, u * EXP:(u + 1) * EXP], xT[:, h, u * P:(u + 1) * P],
                                                routerT[:, h, :], start=h == 0, stop=h == KH - 1)
                        ins.then_inc(logit_mm, 1)
                        pe.reg_add(done, done, 1)
            first_experts(BATCHES - 1, LAST_TILES)
            experts(BATCHES - 1, LAST_TILES)


_INPUTS = ["x", "src", "dst", "edge_type_16", "edge_weight1", "L0_gnn_weight", "L0_gnn_gate_weight",
           "L0_ffn_router_w", "L0_ffn_w1", "L0_ffn_b1", "L0_ffn_w2", "L0_ffn_b2"]


def kernel(**inputs):
    import numpy as np
    import concourse.bacc as bacc
    from concourse import mybir as mb
    from concourse.bass_utils import run_bass_kernel_spmd as run

    nc = bacc.Bacc("TRN2", target_bir_lowering=False, num_devices=1)
    arrays = {"in_" + k: np.ascontiguousarray(inputs[k]) for k in _INPUTS}
    args = [nc.dram_tensor(k, a.shape, mb.dt.from_np(a.dtype), kind="ExternalInput").ap() for k, a in arrays.items()]
    args.append(nc.dram_tensor("out", (N, F), mb.dt.float32, kind="ExternalOutput").ap())
    build(nc, *args)
    return run(nc, [arrays], core_ids=[0]).results[0]["out"]
```

```python
import concourse.bass as bass
from concourse import mybir
from contextlib import ExitStack
from itertools import zip_longest

FP32 = mybir.dt.float32
F32R = mybir.dt.float32r
I32 = mybir.dt.int32
ALU = mybir.AluOpType
ACT = mybir.ActivationFunctionType
AX = mybir.AxisListType

N, E, R, F = 6250, 106250, 16, 256
P = 128
KH = F // P
EXP = 8
TILES = -(-N // P)
LAST_ROWS = N - (TILES - 1) * P
BATCH = 2 * P
BATCHES = -(-N // BATCH)
LAST_TILES = -(-(N - (BATCHES - 1) * BATCH) // P)
NPAD = BATCHES * BATCH
GROUP = 4 * P
GPI = 8
GROUPS = -(-E // GROUP)
ROUNDS = GROUPS // GPI
FULL = E // GROUP
REST = E - FULL * GROUP
WIN = 128
AGGW = NPAD + WIN
STAGE_AT = 18
LAST_SIDE = (BATCHES - 1) % 2 * 2
THIRD = (8, 16)
BIAS_AT = 5
WIN_BANKS = 4
LEAD = 3
SLOTS = 4
EPS = 1e-5
RSQRT_MAGIC = float(0x5F3759DF)
OVER_RES = 2 * BATCHES * F + 4 * 2 * GROUP - 3 * EXP * KH * F
ZERO_TO = OVER_RES + (KH * AGGW - OVER_RES) // 2
assert TILES // 2 - THIRD[1] == EXP and LAST_TILES == 1
assert GROUPS == ROUNDS * GPI and P < FULL < 2 * P


class Chain:

    def __init__(self, engine, sem, base=0):
        self.engine, self.sem, self.base, self.n = engine, sem, base, 0

    def __call__(self, instruction, wait=True):
        instruction.then_inc(self.sem, 1)
        self.n += 1
        if wait:
            self.engine.wait_ge(self.sem, self.base + self.n)

    def link(self, instruction, wait=True):
        instruction.then_inc(self.sem, 1)
        self.n += 1
        yield
        if wait:
            self.engine.wait_ge(self.sem, self.base + self.n)


def alone(chain):
    for _ in chain:
        pass


def woven(first, second, ahead):
    for _ in zip(range(ahead), first):
        pass
    for _ in zip_longest(first, second):
        pass


def build(nc, x, src, dst, etype, eweight, gw, ggate, router, w1, b1, w2, b2, out):
    assert GPI * 4 * F == R * F * 2
    table = nc.dram_tensor("message_table", (N * R, F), FP32, kind="Internal").ap()
    group_dram = nc.dram_tensor("group_numbers", (2 * P, 2), FP32, kind="Internal").ap()
    ctx = ExitStack()
    with ctx:
        def sb(name, shape, dt=FP32):
            return ctx.enter_context(nc.sbuf_tensor(name, shape, dt))

        def sem(name):
            return ctx.enter_context(nc.semaphore(name))

        with ExitStack() as first_part:
            def sb1(name, shape, dt=F32R):
                return first_part.enter_context(nc.sbuf_tensor(name, shape, dt))
            raw = sb1("raw", [P, 4, 2, GROUP], FP32)
            res = sb1("res", [P, 2 * BATCHES, F], FP32)
            w_high = sb1("w_high", [P, R // 2, KH, 2 * F])
            hT = sb1("hT", [P, 2, KH, P])
            gateT = sb1("gateT", [P, KH, 2 * R])
            w_low = sb1("w_low", [P, R // 2, KH, 2 * F])
            hT_low = sb1("hT_low", [P, 2, KH, P])
        staged = res[:, STAGE_AT:STAGE_AT + 4 * R // 2, :].rearrange("p (q h r) o -> p q h (r o)", q=R // 2, h=KH)
        w1_high = sb("w1_high", [P, EXP, KH, F], F32R)
        w1_low = sb("w1_low", [P, EXP, KH, F], F32R)
        w2s = sb("w2s", [P, EXP, KH, F])
        agg = sb("agg", [P, KH * AGGW])
        aggv = agg[:, :].rearrange("p (h n) -> p h n", h=KH)
        xT = sb("xT", [P, KH, BATCH], F32R)
        xT_low = sb("xT_low", [P, KH, BATCH], F32R)
        aggS = sb("aggS", [P, KH, BATCH])
        xres = sb("xres", [P, 4, F])
        S = sb("S", [P, SLOTS, 4, WIN])
        hid = sb("hid", [P, 2, KH, BATCH])
        sb("unused", [P, (8 * GROUP + 2 * BATCHES * F + 2 * KH * R * F + 4 * KH * P + 2 * KH * R)
                      - (3 * EXP * KH * F + KH * AGGW + 3 * KH * BATCH + 4 * F + SLOTS * 4 * WIN + 2 * KH * BATCH)])
        rows = sb("rows", [P, 2, R * F])
        ring = rows[:, :, :].rearrange("p u (s f) -> p (u s) f", f=F)
        b2s = sb("b2s", [EXP, F])
        ident = sb("ident", [P, P])
        small = sb("small", [P, F])
        smallT = sb("smallT", [P, KH, P])
        routerT = sb("routerT", [P, KH, 2 * EXP], F32R)
        gate_sum = sb("gate_sum", [P, 2, R])
        hn = sb("hn", [P, 2, F])
        gate = sb("gate", [P, 2, R])
        stat = sb("stat", [P, 2, 6])
        mv = sb("mv", [P, 2, 2])
        var = sb("var", [P, 2])
        ybits = sb("ybits", [P, 2], I32)
        rstd = sb("rstd", [P, 2])
        tmp = sb("tmp", [P, 2])
        keyT = sb("keyT", [P, GROUPS, 4], I32)
        relT = sb("relT", [P, GROUPS, 4])
        wT = sb("wT", [P, GROUPS, 4])
        idx = sb("idx", [P, 2, GPI * 4], I32)
        iotai = sb("iotai", [P, WIN], I32)
        iota = sb("iota", [P, WIN])
        red = sb("red", [P, 2])
        span = sb("span", [P, 2, 2])
        acc = sb("acc", [P, 2, F])
        grow = acc[0:1, :, :].rearrange("o u f -> o (u f)").rearrange("o (g k) -> o g k", k=2)
        w1_stage = acc[:, :, :]
        scan = sb("scan", [1, 2, 64])
        half = sb("half", [1, 2, GPI // 2 * ROUNDS])
        tab = sb("tab", [1, ROUNDS + 1, 4 + GPI], I32)
        tokS = hn
        logits = sb("logits", [P, 2, EXP])
        lg = sb("lg", [P, 2, EXP])
        pr = sb("pr", [P, 2, EXP])
        rank = sb("rank", [P, 2, EXP])
        comb = sb("comb", [P, 2, EXP])
        cmp = sb("cmp", [P, 2, EXP, EXP])
        cmp2 = sb("cmp2", [P, 2, EXP, EXP])
        lower = sb("lower", [P, EXP, EXP])
        col = sb("col", [P, 2])
        top = sb("top", [P, 2])
        combT = sb("combT", [EXP, 2, P])
        bank = [ctx.enter_context(nc.psum_tensor(f"bank{n}", [P, 512], FP32)) for n in range(8)]

        x_in = [sem(f"x_in{n}") for n in range(5)]
        small_in, b2_in, raw_in, grow_in = sem("small_in"), sem("b2_in"), sem("raw_in"), sem("grow_in")
        w_in = [sem(f"w_in{n}") for n in range(8)]
        exp_in, w1_in, x2_in = sem("exp_in"), sem("w1_in"), sem("x2_in")
        w1_high_ok, w1_low_ok, xT_low_ok = sem("w1_high_ok"), sem("w1_low_ok"), sem("xT_low_ok")
        table_out = [sem("table_out0"), sem("table_out1")]
        rows_free = sem("rows_free")
        pool_chain = sem("pool_chain")
        ident_ok, small_zero, raw_zero, edges_ok, tabs_ok = (
            sem("ident_ok"), sem("small_zero"), sem("raw_zero"), sem("edges_ok"), sem("tabs_ok"))
        extremes_ok = sem("extremes_ok")
        span_ok, span_out, tab_chain = sem("span_ok"), sem("span_out"), sem("tab_chain")
        iota_ok = sem("iota_ok")
        small_tr, small_ok = sem("small_tr"), sem("small_ok")
        res_zero = sem("res_zero")
        ln_chain, ln_pair = sem("ln_chain"), sem("ln_pair")
        w_high_ok, w_low_ok, hT_low_ok = sem("w_high_ok"), sem("w_low_ok"), sem("hT_low_ok")
        tr_done, hT_ok, gate_mm, gate_ok = sem("tr_done"), sem("hT_ok"), sem("gate_mm"), sem("gate_ok")
        mm_done, evac_act, evac_dve = sem("mm_done"), sem("evac_act"), sem("evac_dve")
        edge_tr, edge_ev = sem("edge_tr"), [sem("edge_act"), sem("edge_dve")]
        agg_zero, agg_zero_act, agg_zero_pool = sem("agg_zero"), sem("agg_zero_act"), sem("agg_zero_pool")
        turn_free = sem("turn_free")
        idx_ok = sem("idx_ok")
        gate_sum_ok = sem("gate_sum_ok")
        gathered = [sem(f"gathered{r}") for r in range(GPI)]
        S_ok, seg_mm, added, shifted = sem("S_ok"), sem("seg_mm"), sem("added"), sem("shifted")
        relu_ok, agg_tr, tok_chain, tok_ok, tok_tr, xT_ok = (
            sem("relu_ok"), sem("agg_tr"), sem("tok_chain"), sem("tok_ok"), sem("tok_tr"), sem("xT_ok"))
        logit_mm, exp_ready, exp_ok, route_chain = (
            sem("logit_mm"), sem("exp_ready"), sem("exp_ok"), sem("route_chain"))
        comb_ok, top_ok = sem("comb_ok"), sem("top_ok")
        comb_tr, combT_ok, bias_mm, acc_done = sem("comb_tr"), sem("combT_ok"), sem("bias_mm"), sem("acc_done")
        h_mm, hid_ok, y_mm, y_added = sem("h_mm"), sem("hid_ok"), sem("y_mm"), sem("y_added")
        out_done, acc_free = sem("out_done"), sem("acc_free")
        bias_added = sem("bias_added")
        hold = sem("hold")

        def round_numbers(engine, i, registers):
            engine.load(registers, tab[0:1, bass.ds(i, 1), 0:len(registers)].rearrange("o r k -> o (r k)"))
            return (engine.snap(registers[0], min_val=0, max_val=NPAD // WIN),
                    engine.snap(registers[1], min_val=0, max_val=BATCHES),
                    engine.snap(registers[2], min_val=0, max_val=BATCHES))

        Y_BANK = [bank[n] for n in (4, 5, 0, 1, 4, 5, 4, 5)]
        Y_BEFORE = (None, None, None, None, 0, 1, 4, 5)

        block = ctx.enter_context(nc.Block())

        @block.sync
        def _(sp):
            def load_x(n, t0, t1):
                sp.dma_start(res[:, t0:t1, :], x[t0 * P:t1 * P, :].rearrange("(t p) f -> p t f", p=P)
                             ).then_inc(x_in[n], 16)
            sp.sem_inc(rows_free, 2)
            load_x(0, 0, 4)
            sp.wait_ge(small_zero, 1)
            sp.dma_start(small[0:R, :], ggate.rearrange("r f o -> r (f o)")).then_inc(small_in, 16)
            sp.dma_start(small[32:32 + EXP, :], router).then_inc(small_in, 16)
            sp.dma_start(small[64:64 + EXP * KH, 0:P], b1.rearrange("e (h p) -> (e h) p", p=P)).then_inc(small_in, 16)
            for n in range(8):
                for h in range(KH):
                    sp.dma_start(staged[:, n, h, :].rearrange("p (r o) -> p r o", r=2),
                                 gw[2 * n:2 * n + 2, h * P:(h + 1) * P, :].rearrange("r p o -> p r o")
                                 ).then_inc(w_in[n], 16)
            load_x(1, 4, STAGE_AT)
            sp.wait_ge(raw_zero, 1)
            for a, arr in enumerate((src, dst, etype, eweight)):
                flat = arr if a < 3 else arr.rearrange("e o -> (e o)")
                view = raw[:, a, :, :] if a == 3 else raw[:, a, :, :].bitcast(I32)
                sp.dma_start(view[:, 0, :], flat[0:P * GROUP].rearrange("(q e) -> q e", q=P)).then_inc(raw_in, 16)
                sp.dma_start(view[0:FULL - P, 1, :], flat[P * GROUP:FULL * GROUP].rearrange("(q e) -> q e", e=GROUP)
                             ).then_inc(raw_in, 16)
                sp.dma_start(view[FULL - P:FULL - P + 1, 1, 0:REST], flat[FULL * GROUP:E].rearrange("(q e) -> q e", q=1)
                             ).then_inc(raw_in, 16)
            sp.wait_ge(w_low_ok, R // 2)
            load_x(2, STAGE_AT, 34)
            load_x(3, 34, TILES - 1)
            sp.wait_ge(res_zero, 1)
            sp.dma_start(res[0:LAST_ROWS, TILES - 1, :], x[(TILES - 1) * P:N, :]).then_inc(x_in[4], 16)
            sp.dma_start(b2s[:, :], b2).then_inc(b2_in, 16)

            def write_half(slot, q2, node, count, rows_n=P):
                sp.wait_ge(evac_act, count)
                sp.wait_ge(evac_dve, count)
                span_ = R * F // 2
                dstv = table[bass.ds(node * R, rows_n * R), :].rearrange("(n r) f -> n (r f)", r=R)
                sp.dma_start(dstv[:, q2 * span_:(q2 + 1) * span_], rows[0:rows_n, slot, q2 * span_:(q2 + 1) * span_]
                             ).then_inc(table_out[slot], 16)

            def write_tiles(i0, i1):
                with sp.Fori(0, i1 - i0) as k:
                    i = k + i0
                    write_half(0, 0, i * (2 * P), i * 8 + 4)
                    if i0 == THIRD[1]:
                        sp.wait_ge(w1_low_ok, k + 1)
                        sp.dma_start(w1_stage, w1[bass.ds(k, 1), :, :].rearrange("e (h p) o -> p (e h) o", p=P)
                                     ).then_inc(w1_in, 16)
                    write_half(0, 1, i * (2 * P), i * 8 + 6)
                    write_half(1, 0, i * (2 * P) + P, i * 8 + 8)
                    sp.wait_ge(table_out[0], i * 32 + 32)
                    sp.sem_inc(rows_free, 1)
                    write_half(1, 1, i * (2 * P) + P, i * 8 + 10)
                    sp.wait_ge(table_out[1], i * 32 + 32)
                    sp.sem_inc(rows_free, 1)

            write_tiles(0, THIRD[1])
            for h in range(KH):
                sp.dma_start(w2s[:, :, h, :], w2[:, h * P:(h + 1) * P, :].rearrange("e p o -> p e o")
                             ).then_inc(exp_in, 16)
            write_tiles(THIRD[1], TILES // 2)
            write_half(0, 0, (TILES - 1) * P, (TILES - 1) * 4 + 4, LAST_ROWS)
            write_half(0, 1, (TILES - 1) * P, (TILES - 1) * 4 + 6, LAST_ROWS)
            sp.wait_ge(mm_done, 8 * TILES + 16)
            for b in range(2):
                sp.dma_start(xres[:, 2 * b:2 * b + 2, :],
                             x[b * BATCH:(b + 1) * BATCH, :].rearrange("(u p) f -> p u f", p=P)).then_inc(x2_in, 16)
                sp.wait_ge(x2_in, b * 16 + 16)

            sent = sp.alloc_register("sent")
            sp.reg_mov(sent, 0)
            side, other = sp.alloc_register("side"), sp.alloc_register("other")
            sp.reg_mov(side, 0)
            sp.reg_mov(other, 2)
            kept = sp.alloc_register("place")
            row = [sp.alloc_register(f"row{k}") for k in range(4)]
            sp.sem_inc(acc_free, 1)
            sp.wait_ge(tabs_ok, 1)
            with sp.Fori(0, ROUNDS) as i:
                _, lo, hi = round_numbers(sp, i, row)
                first = sp.snap((lo < 1) * 1 + lo, min_val=0, max_val=BATCHES)
                with sp.If(first < hi):
                    with sp.Fori(first, hi):
                        b = sp.snap(sent, min_val=0, max_val=BATCHES - 2)
                        sp.wait_ge(acc_done, b + 2)
                        sp.dma_start(out[bass.ds(b * BATCH, BATCH), :].rearrange("(u p) f -> p u f", p=P),
                                     acc[:, :, :]).then_inc(out_done, 16)
                        place = sp.snap(side, min_val=0, max_val=2)
                        with sp.If(b < BATCHES - 3):
                            early = sp.snap(sent, min_val=0, max_val=BATCHES - 4)
                            sp.dma_start(xres[:, bass.ds(place, 2), :],
                                         x[bass.ds(early * BATCH + 2 * BATCH, BATCH), :].rearrange("(u p) f -> p u f", p=P)
                                         ).then_inc(x2_in, 16)
                        with sp.If(b > BATCHES - 4):
                            with sp.If(b < BATCHES - 2):
                                sp.dma_start(xres[0:LAST_ROWS, LAST_SIDE, :], x[(BATCHES - 1) * BATCH:N, :]
                                             ).then_inc(x2_in, 16)
                        sp.reg_mov(kept, side)
                        sp.reg_mov(side, other)
                        sp.reg_mov(other, kept)
                        sp.wait_ge(out_done, b * 16 + 16)
                        sp.sem_inc(acc_free, 1)
                        sp.reg_add(sent, sent, 1)
            sp.wait_ge(acc_done, BATCHES + 1)
            left = N - (BATCHES - 1) * BATCH
            for u in range(2):
                n0 = (BATCHES - 1) * BATCH + u * P
                n1 = min(n0 + P, N)
                if n1 > n0:
                    sp.dma_start(out[n0:n1, :], acc[0:n1 - n0, u, :]).then_inc(out_done, 16)
            sp.wait_ge(out_done, 16 * (BATCHES - 1) + 16 * (-(-left // P)))

        @block.gpsimd
        def _(pool):
            chain = Chain(pool, pool_chain)
            chain(pool.memset(small[:, :], 0.0))
            pool.sem_inc(small_zero, 1)
            chain(pool.memset(ident[:, :], 0.0))
            pool.affine_select(out=ident[:, :], in_=ident[:, :], compare_op=ALU.not_equal, fill=1.0, base=0,
                               pattern=[[-1, P]], channel_multiplier=1).then_inc(ident_ok, 1)
            pool.memset(raw[:, 0, 1, :].bitcast(I32), 0)
            pool.memset(raw[:, 1, 1, :].bitcast(I32), N - 1)
            pool.memset(raw[:, 2, 1, :].bitcast(I32), 0)
            pool.memset(raw[:, 3, 1, :], 0.0).then_inc(raw_zero, 1)
            pool.iota(iotai[:, :], pattern=[[1, WIN]], base=0, channel_multiplier=0).then_inc(iota_ok, 1)
            pool.wait_ge(iota_ok, 1)
            pool.tensor_copy(iota[:, :], iotai[:, :]).then_inc(iota_ok, 1)
            chain(pool.memset(lower[:, :, :], 1.0))
            chain(pool.affine_select(out=lower[:, :, :], in_=lower[:, :, :], compare_op=ALU.is_gt, fill=0.0, base=0,
                                     pattern=[[1, EXP], [-1, EXP]], channel_multiplier=0))
            pool.wait_ge(span_ok, 1)
            chain(pool.tensor_copy(raw[:, 1, :, :], raw[:, 1, :, :].bitcast(I32)))
            for b in range(2):
                chain(pool.tensor_scalar(raw[:, 1, b, :], raw[:, 1, b, :], span[:, b, 0:1], None, ALU.subtract))
            chain(pool.tensor_scalar(raw[:, 0, :, :], raw[:, 0, :, :].bitcast(I32), float(R), None, ALU.mult))
            chain(pool.tensor_copy(raw[:, 2, :, :], raw[:, 2, :, :].bitcast(I32)))
            pool.tensor_tensor(raw[:, 0, :, :], raw[:, 0, :, :], raw[:, 2, :, :], ALU.add
                               ).then_inc(edges_ok, 1)
            pool.dma_start(group_dram.rearrange("(b q) k -> q b k", q=P), span[:, :, :]).then_inc(span_out, 16)
            pool.wait_ge(span_out, 16)
            pool.dma_start(grow[:, :, :], group_dram.rearrange("(o g) k -> o g k", o=1)).then_inc(grow_in, 16)

            pool.wait_ge(edge_ev[0], 3)
            pool.wait_ge(edge_ev[1], 3)
            pool.wait_ge(ln_pair, TILES + 1)
            pool.memset(agg[:, 0:OVER_RES], 0.0).then_inc(agg_zero_pool, 1)
            pool.wait_ge(table_out[0], 32 * (TILES // 2 + 1))
            pool.wait_ge(table_out[1], 32 * (TILES // 2))
            pool.sem_inc(hold, 1)
            passes = pool.alloc_register("passes")
            pool.reg_mov(passes, 0)
            with pool.Fori(0, ROUNDS // 2) as i:
                for h in range(2):
                    extra = pool.value_load(tab[0:1, bass.ds(i * 2 + h, 1), 0:1].rearrange("o r k -> o (r k)"),
                                            min_val=0, max_val=NPAD // WIN)
                    p = pool.snap(passes, min_val=0, max_val=1 << 20)
                    pool.wait_ge(seg_mm, p * GPI + 1)
                    pool.sem_inc(hold, 1)
                    pool.tensor_copy(idx[:, h, :], keyT[:, bass.ds(i * (2 * GPI) + h * GPI, GPI), :].rearrange("p g j -> p (g j)")
                                     ).then_inc(idx_ok, 1)
                    pool.wait_ge(idx_ok, i * 2 + (h + 1))
                    for r in range(GPI):
                        pool.wait_ge(seg_mm, p * GPI + (r + 1))
                        pool.sem_inc(turn_free, 1)
                        for j in range(4):
                            pool.indirect_dma_start(
                                out=ring[:, r * 4 + j, :], out_offset=None, in_=table[:, :],
                                in_offset=bass.IndirectOffsetOnAxis(ap=idx[:, h, r * 4 + j:r * 4 + j + 1], axis=0),
                            ).then_inc(gathered[r], 16)
                    pool.reg_add(passes, passes, extra + 1)

        @block.scalar
        def _(act):
            act.sem_inc(evac_act, 2)
            act.sem_inc(hT_ok, 2)
            act.sem_inc(gate_ok, 1)
            act.wait_ge(small_tr, 1)
            act.activation(smallT[:, :, :], bank[7][:, 0:KH * P].rearrange("p (h q) -> p h q", h=KH), ACT.Copy
                           ).then_inc(small_ok, 1)
            act.wait_ge(small_ok, 1)
            act.activation(gateT[:, :, 0:R], smallT[:, :, 0:R], ACT.Copy).then_inc(small_ok, 1)
            act.activation(routerT[:, :, 0:EXP], smallT[:, :, 32:32 + EXP], ACT.Copy).then_inc(small_ok, 1)

            def copy_hT(u, t):
                act.wait_ge(tr_done, t + 3)
                act.wait_ge(mm_done, t * 8 + 8)
                act.activation(hT[:, u, :, :], bank[4 + u][:, 0:KH * P].rearrange("p (h q) -> p h q", h=KH), ACT.Copy
                               ).then_inc(hT_ok, 1)

            def gates_and_rows(u, t):
                act.wait_ge(gate_sum_ok, t + 1)
                act.wait_ge(rows_free, t + 1)
                act.activation(gate[:, u, :], gate_sum[:, u, :], ACT.Sigmoid).then_inc(gate_ok, 1)
                act.wait_ge(gate_ok, t + 2)
                for k in range(4):
                    q = 2 * k
                    act.wait_ge(mm_done, t * 8 + (q + 17))
                    for r in range(2):
                        ins = act.activation(rows[:, u, (2 * q + r) * F:(2 * q + r + 1) * F],
                                             bank[q % 4][:, r * F:(r + 1) * F], ACT.Copy,
                                             scale=gate[:, u, 2 * q + r:2 * q + r + 1])
                    ins.then_inc(evac_act, 1)

            copy_hT(0, 0)
            for q in range(R // 2):
                act.wait_ge(w_in[q], 32)
                act.activation(w_high[:, q, :, :], staged[:, q, :, :], ACT.Copy).then_inc(w_high_ok, 1)

            def part1(i0, i1):
                with act.Fori(0, i1 - i0) as e:
                    i = e + i0
                    copy_hT(1, i * 2 + 1)
                    gates_and_rows(0, i * 2)
                    copy_hT(0, i * 2 + 2)
                    gates_and_rows(1, i * 2 + 1)
                    if i0 == THIRD[1]:
                        act.wait_ge(w1_in, e * 16 + 16)
                        act.sem_inc(hold, 1)
                        act.activation(w1_high[:, bass.ds(e, 1), :, :].rearrange("p e h o -> p (e h) o"), w1_stage,
                                       ACT.Copy).then_inc(w1_high_ok, 1)

            part1(0, THIRD[1])
            for n, dst_ in ((0, keyT), (2, relT), (4, wT)):
                act.wait_ge(edge_tr, n + 1)
                act.activation(dst_[:, 0:P, :].rearrange("p g j -> p j g"),
                               bank[7][:, :].rearrange("p (j g) -> p j g", j=4), ACT.Copy).then_inc(edge_ev[0], 1)
            part1(THIRD[1], TILES // 2)
            gates_and_rows(0, TILES - 1)

            act.wait_ge(mm_done, 8 * TILES + 16)
            act.wait_ge(agg_zero_pool, 1)
            act.activation(agg[:, ZERO_TO:KH * AGGW], agg[:, 0:KH * AGGW - ZERO_TO], ACT.Copy).then_inc(agg_zero_act, 1)
            act.sem_inc(hid_ok, 2)
            act.wait_ge(tabs_ok, 1)
            done = act.alloc_register("batches")
            act.reg_mov(done, 0)
            row = [act.alloc_register(f"row{k}") for k in range(4)]
            mixed = act.alloc_register("mixed")
            act.reg_mov(mixed, 0)

            def experts(b, tiles=2):
                for e in range(EXP):
                    act.wait_ge(h_mm, b * EXP + (e + 1))
                    act.wait_ge(y_mm, b * EXP + (e + 1))
                    for h in range(KH):
                        ins = act.activation(hid[:, e % 2, h, 0:tiles * P],
                                             bank[2 + e % 2][:, h * BATCH:h * BATCH + tiles * P],
                                             ACT.Gelu, bias=smallT[:, 0, 64 + e * KH + h:65 + e * KH + h])
                    ins.then_inc(hid_ok, 1)

            with act.Fori(0, ROUNDS) as i:
                _, lo, hi = round_numbers(act, i, row)
                with act.If(lo < hi):
                    with act.Fori(lo, hi):
                        f = act.snap(done, min_val=0, max_val=BATCHES - 1)
                        with act.If(f > 0):
                            experts(act.snap(mixed, min_val=0, max_val=BATCHES - 2))
                            act.reg_add(mixed, mixed, 1)
                        act.wait_ge(tok_tr, f + 1)
                        act.activation(xT[:, :, :], bank[6][:, :].rearrange("p (h n) -> p h n", h=KH), ACT.Copy
                                       ).then_inc(xT_ok, 1)
                        act.wait_ge(exp_ready, f + 1)
                        act.activation(pr[:, :, :], lg[:, :, :], ACT.Exp).then_inc(exp_ok, 1)
                        act.reg_add(done, done, 1)
            experts(BATCHES - 1, LAST_TILES)

        @block.vector
        def _(dve):
            dve.sem_inc(evac_dve, 2)
            dve.sem_inc(hT_low_ok, 2)
            dve.sem_inc(w1_low_ok, 1)

            def rstd_of(chain, width):
                v, y, t = var[:, 0:width], rstd[:, 0:width], tmp[:, 0:width]
                yield from chain.link(dve.tensor_scalar(v, mv[:, 0:width, 1], EPS, None, ALU.add))
                yield from chain.link(dve.tensor_scalar(ybits[:, 0:width], v.bitcast(I32), 1, None, ALU.arith_shift_right))
                yield from chain.link(dve.tensor_scalar(y.bitcast(I32), ybits[:, 0:width], -1.0, RSQRT_MAGIC, ALU.mult, ALU.add))
                for _ in range(3):
                    yield from chain.link(dve.scalar_tensor_tensor(t, y, -0.5, y, ALU.mult, ALU.mult))
                    yield from chain.link(dve.tensor_tensor(t, t, v, ALU.mult))
                    yield from chain.link(dve.scalar_tensor_tensor(y, t, 1.5, y, ALU.add, ALU.mult))

            def stats(chain, tile):
                for u in range(2):
                    dve.sem_inc(hold, 1)
                    yield from chain.link(dve.bn_stats(stat[:, u, :], tile(u)), wait=u == 1)
                for u in range(2):
                    dve.sem_inc(hold, 1)
                    yield from chain.link(dve.bn_aggr(mv[:, u, :], stat[:, u, :]), wait=u == 1)
                yield from rstd_of(chain, 2)

            def norm_pair(chain, t):
                for u in range(2):
                    dve.wait_ge(tr_done, t + (1 + u))
                    dve.sem_inc(hold, 1)
                    dve.tensor_scalar(hn[:, u, :], res[:, bass.ds(t + u, 1), :].rearrange("p o f -> p (o f)"),
                                      mv[:, u, 0:1], rstd[:, u:u + 1], ALU.subtract, ALU.mult).then_inc(ln_pair, 1)

            def rows_of(t):
                return lambda u: res[:, bass.ds(t + u, 1), :].rearrange("p o f -> p (o f)")

            def evacuate(u, t, k):
                q = 2 * k + 1
                dve.wait_ge(mm_done, t * 8 + (q + 17))
                dve.tensor_tensor(rows[:, u, 2 * q * F:(2 * q + 2) * F].rearrange("p (r f) -> p r f", r=2),
                                  bank[q % 4][:, :].rearrange("p (r f) -> p r f", r=2),
                                  gate[:, u, 2 * q:2 * q + 2].unsqueeze(2).to_broadcast([P, 2, F]), ALU.mult
                                  ).then_inc(evac_dve, 1)

            def low_hT(u, t):
                dve.wait_ge(hT_ok, t + 3)
                dve.tensor_tensor(hT_low[:, u, :, :], bank[4 + u][:, 0:KH * P].rearrange("p (h q) -> p h q", h=KH),
                                  hT[:, u, :, :].bitcast(FP32), ALU.subtract).then_inc(hT_low_ok, 1)

            def sum_gates(u, t):
                dve.wait_ge(gate_mm, t + 1)
                dve.tensor_reduce(gate_sum[:, u, :], bank[6][:, 0:2 * R].rearrange("p (k r) -> p r k", k=2), AX.X, ALU.add
                                  ).then_inc(gate_sum_ok, 1)

            LINKS = 4 + 3 + 9
            dve.wait_ge(x_in[0], 16)
            first = Chain(dve, ln_chain)
            alone(stats(first, rows_of(0)))
            norm_pair(None, 0)
            assert first.n == LINKS
            dve.wait_ge(small_ok, 3)
            dve.tensor_tensor(routerT[:, :, EXP:2 * EXP], smallT[:, :, 32:32 + EXP], routerT[:, :, 0:EXP].bitcast(FP32),
                              ALU.subtract).then_inc(small_ok, 1)
            dve.tensor_tensor(gateT[:, :, R:2 * R], smallT[:, :, 0:R], gateT[:, :, 0:R].bitcast(FP32), ALU.subtract
                              ).then_inc(small_ok, 1)
            low_hT(0, 0)
            for q in range(R // 2):
                dve.wait_ge(w_high_ok, q + 1)
                dve.tensor_tensor(w_low[:, q, :, :], staged[:, q, :, :], w_high[:, q, :, :].bitcast(FP32), ALU.subtract
                                  ).then_inc(w_low_ok, 1)
            dve.wait_ge(w_low_ok, R // 2)
            dve.memset(res[:, TILES - 1:2 * BATCHES, :], 0.0).then_inc(res_zero, 1)

            def part1(i0, i1):
                with dve.Fori(0, i1 - i0) as e:
                    i = e + i0
                    for u in range(2):
                        t = i * 2 + u
                        sum_gates(u, t)
                        low_hT(1 - u, t + 1)
                        dve.wait_ge(gate_ok, t + 2)
                        dve.wait_ge(rows_free, t + 1)
                        for k in range(4):
                            evacuate(u, t, k)
                            if u == 0 and k == 0:
                                c = Chain(dve, ln_chain, (i + 1) * LINKS)
                                dve.wait_ge(ln_pair, i * 2 + 2)
                                alone(stats(c, rows_of(i * 2 + 2)))
                                assert c.n == LINKS
                            if u == 0 and k == 1:
                                norm_pair(None, i * 2 + 2)
                            if u == 1 and k == 3 and i0 == THIRD[1]:
                                dve.wait_ge(w1_high_ok, e + 1)
                                dve.sem_inc(hold, 1)
                                dve.tensor_tensor(w1_low[:, bass.ds(e, 1), :, :].rearrange("p e h o -> p (e h) o"), w1_stage,
                                                  w1_high[:, bass.ds(e, 1), :, :].rearrange("p e h o -> p (e h) o").bitcast(FP32),
                                                  ALU.subtract).then_inc(w1_low_ok, 1)
                    dve.wait_ge(x_in[1], 16)

            part1(0, THIRD[0])
            dve.wait_ge(raw_in, 12 * 16)
            dve.tensor_reduce(span[:, :, 0], raw[:, 1, :, :].bitcast(I32), AX.X, ALU.min).then_inc(extremes_ok, 1)
            dve.tensor_reduce(red[:, :], raw[:, 1, :, :].bitcast(I32), AX.X, ALU.max).then_inc(extremes_ok, 1)
            dve.wait_ge(extremes_ok, 2)
            dve.tensor_tensor(span[:, :, 1], red[:, :], span[:, :, 0], ALU.subtract).then_inc(span_ok, 1)
            dve.wait_ge(x_in[2], 16)
            part1(THIRD[0], THIRD[1])
            for n, dst_ in ((1, keyT), (3, relT), (5, wT)):
                dve.wait_ge(edge_tr, n + 1)
                dve.tensor_copy(dst_[:, P:GROUPS, :].rearrange("p g j -> p j g"),
                                bank[6][:, :].rearrange("p (j g) -> p j g", j=4)[:, :, 0:GROUPS - P]).then_inc(edge_ev[1], 1)
            chain = Chain(dve, tab_chain)
            dve.wait_ge(grow_in, 16)
            lows, spans = grow[0:1, 0:GROUPS, 0], grow[0:1, 0:GROUPS, 1]
            chain(dve.memset(tab[0:1, :, :], 0))
            chain(dve.tensor_copy(tab[0:1, 0:ROUNDS, 4:4 + GPI], lows.rearrange("o (r g) -> o r g", g=GPI)))

            def over_groups(v, k, op):
                a = v.rearrange("o (r g) -> o r g", g=GPI)
                n = GPI // 2
                dst_ = half[0:1, k, :].rearrange("o (r g) -> o r g", g=n)
                chain(dve.tensor_tensor(dst_, a[:, :, 0:n], a[:, :, n:2 * n], op))
                while n > 1:
                    n //= 2
                    chain(dve.tensor_tensor(dst_[:, :, 0:n], dst_[:, :, 0:n], dst_[:, :, n:2 * n], op))
                return dst_[:, :, 0]
            widest = over_groups(spans, 0, ALU.max)
            chain(dve.tensor_scalar(tab[0:1, 0:ROUNDS, 0], widest, 1.0 / WIN, 0.5 / WIN - 0.5, ALU.mult, ALU.add))
            lowest = over_groups(lows, 1, ALU.min)
            chain(dve.memset(scan[0:1, :, :], float(NPAD)))
            chain(dve.tensor_copy(scan[0:1, 0, 0:ROUNDS - 1], lowest[:, 1:ROUNDS]))
            step, k = 1, 0
            while step < ROUNDS:
                chain(dve.tensor_tensor(scan[0:1, 1 - k, 0:ROUNDS], scan[0:1, k, 0:ROUNDS],
                                         scan[0:1, k, step:step + ROUNDS], ALU.min))
                step, k = 2 * step, 1 - k
            for at, count, c in ((0, ROUNDS, 2), (1, ROUNDS - 1, 1)):
                chain(dve.tensor_scalar(tab[0:1, at:ROUNDS, c], scan[0:1, k, 0:count], 1.0 / BATCH,
                                        0.5 / BATCH - 0.5, ALU.mult, ALU.add))
            dve.sem_inc(tabs_ok, 1)
            dve.wait_ge(x_in[3], 16)
            dve.wait_ge(x_in[4], 16)
            part1(THIRD[1], TILES // 2)
            sum_gates(0, TILES - 1)
            dve.wait_ge(gate_ok, TILES + 1)
            dve.wait_ge(rows_free, TILES)
            for k in range(4):
                evacuate(0, TILES - 1, k)

            dve.wait_ge(mm_done, 8 * TILES + 16)
            dve.memset(agg[:, OVER_RES:ZERO_TO], 0.0).then_inc(agg_zero, 1)
            dve.sem_inc(added, WIN_BANKS)
            dve.sem_inc(shifted, 1)
            dve.sem_inc(y_added, 2)
            dve.sem_inc(acc_done, 1)
            dve.sem_inc(bias_added, 1)
            dve.wait_ge(tabs_ok, 1)
            dve.wait_ge(iota_ok, 2)
            dve.wait_ge(edge_ev[0], 3)
            dve.wait_ge(edge_ev[1], 3)
            dve.wait_ge(agg_zero, 1)
            dve.wait_ge(agg_zero_act, 1)
            passes = dve.alloc_register("passes")
            done = dve.alloc_register("batches")
            base = dve.alloc_register("base")
            following = dve.alloc_register("following")
            side, other = dve.alloc_register("side"), dve.alloc_register("other")
            kept = dve.alloc_register("kept")
            dve.reg_mov(side, 0)
            dve.reg_mov(other, 2)

            def sums(place):
                return lambda u: xres[:, bass.ds(place + u, 1), :].rearrange("p o f -> p (o f)")
            row = [dve.alloc_register(f"row{k}") for k in range(4 + GPI)]
            dve.reg_mov(passes, 0)
            dve.reg_mov(done, 0)
            mixed = dve.alloc_register("mixed")
            dve.reg_mov(mixed, 0)

            def combT_copy(b):
                dve.wait_ge(comb_tr, b + 2)
                dve.tensor_copy(combT[:, :, :], bank[7][0:EXP, 0:2 * P].rearrange("e (u p) -> e u p", u=2)
                                ).then_inc(combT_ok, 1)

            def experts(b, place, tiles=2, between=()):
                dve.wait_ge(acc_free, b + 1)
                for e in range(EXP):
                    if e == 2:
                        combT_copy(b)
                    for at, step in between:
                        if e == at:
                            step()
                    dve.wait_ge(y_mm, b * EXP + (e + 3))
                    for u in range(tiles):
                        dve.wait_ge(y_added, b * (2 * EXP) + (tiles * (e - 1) + u + 3))
                        if e == 0:
                            dve.sem_inc(hold, 1)
                        before = sums(place)(u) if e == 0 else acc[:, u, :]
                        dve.scalar_tensor_tensor(acc[:, u, :], Y_BANK[e][:, u * F:(u + 1) * F],
                                                 comb[:, u, e:e + 1], before, ALU.mult, ALU.add
                                                 ).then_inc(y_added, 1)
                    if e == BIAS_AT:
                        dve.wait_ge(bias_mm, b + 1)
                        dve.wait_ge(y_added, b * (2 * EXP) + (tiles * (e + 1) + 2))
                        dve.tensor_tensor(acc[:, 0:tiles, :], acc[:, 0:tiles, :],
                                          bank[7][:, 0:tiles * F].rearrange("p (u f) -> p u f", u=tiles), ALU.add).then_inc(bias_added, 1)
                        dve.wait_ge(bias_added, b + 2)
                dve.wait_ge(y_added, b * (2 * EXP) + (tiles * EXP + 2))
                dve.sem_inc(acc_done, 1)

            TOK_LINKS = 1 + LINKS
            ROUTE_LINKS = 2 + 6 + 5

            def tokens(f, place):
                c = Chain(dve, tok_chain, f * TOK_LINKS)
                pair = xres[:, bass.ds(place, 2), :]
                dve.wait_ge(x2_in, f * 16 + 16)
                dve.wait_ge(agg_tr, f + 2)
                dve.sem_inc(hold, 1)
                yield from c.link(dve.tensor_tensor(pair, bank[6][:, :].rearrange("p (u f) -> p u f", u=2), pair, ALU.add))
                yield from stats(c, sums(place))
                for u in range(2):
                    dve.tensor_scalar(tokS[:, u, :], sums(place)(u), mv[:, u, 0:1], rstd[:, u:u + 1],
                                      ALU.subtract, ALU.mult).then_inc(tok_ok, 1)
                assert c.n == TOK_LINKS
            def shift_logits(f):
                dve.wait_ge(logit_mm, f + 1)
                parts = bank[7][:, 0:4 * EXP].rearrange("p (u k e) -> p u e k", u=2, k=2)
                dve.tensor_reduce(logits[:, :, :], parts, AX.X, ALU.add).then_inc(top_ok, 1)
                dve.wait_ge(top_ok, f * 2 + 1)
                dve.tensor_reduce(top[:, :], logits[:, :, :], AX.X, ALU.max).then_inc(top_ok, 1)
                dve.wait_ge(top_ok, f * 2 + 2)
                dve.tensor_tensor(lg[:, :, :], logits[:, :, :], top[:, :].unsqueeze(2).to_broadcast([P, 2, EXP]), ALU.subtract
                                  ).then_inc(exp_ready, 1)

            def route(f):
                c = Chain(dve, route_chain, f * ROUTE_LINKS)
                dve.wait_ge(exp_ok, f + 1)
                yield from c.link(dve.tensor_reduce(col[:, :], pr[:, :, :], AX.X, ALU.add))
                yield from c.link(dve.reciprocal(col[:, :], col[:, :]))
                yield from c.link(dve.tensor_tensor(pr[:, :, :], pr[:, :, :], col[:, :].unsqueeze(2).to_broadcast([P, 2, EXP]), ALU.mult))
                pj = pr[:, :, :].unsqueeze(2).to_broadcast([P, 2, EXP, EXP])
                pe_ = pr[:, :, :].unsqueeze(3).to_broadcast([P, 2, EXP, EXP])
                low_ = lower[:, :, :].unsqueeze(1).to_broadcast([P, 2, EXP, EXP])
                yield from c.link(dve.tensor_tensor(cmp[:, :, :, :], pj, pe_, ALU.is_gt), wait=False)
                yield from c.link(dve.tensor_tensor(cmp2[:, :, :, :], pj, pe_, ALU.is_equal))
                yield from c.link(dve.tensor_tensor(cmp2[:, :, :, :], cmp2[:, :, :, :], low_, ALU.mult))
                yield from c.link(dve.tensor_tensor(cmp[:, :, :, :], cmp[:, :, :, :], cmp2[:, :, :, :], ALU.add))
                yield from c.link(dve.tensor_reduce(rank[:, :, :], cmp[:, :, :, :], AX.X, ALU.add))
                yield from c.link(dve.scalar_tensor_tensor(pr[:, :, :], rank[:, :, :], 1.5, pr[:, :, :], ALU.is_lt, ALU.mult))
                yield from c.link(dve.tensor_reduce(col[:, :], pr[:, :, :], AX.X, ALU.add))
                yield from c.link(dve.tensor_scalar(col[:, :], col[:, :], 1e-12, None, ALU.max))
                yield from c.link(dve.reciprocal(col[:, :], col[:, :]))
                dve.wait_ge(y_added, f * (2 * EXP) + 2)
                dve.wait_ge(comb_tr, f + 1)
                yield from c.link(dve.tensor_tensor(comb[:, :, :], pr[:, :, :], col[:, :].unsqueeze(2).to_broadcast([P, 2, EXP]), ALU.mult))
                assert c.n == ROUTE_LINKS, c.n
                dve.sem_inc(comb_ok, 1)

            def weights_by_target(slot, g, seg_count):
                dve.wait_ge(seg_mm, seg_count)
                dve.sem_inc(hold, 1)
                for j in range(4):
                    ins = dve.tensor_scalar(S[:, slot % SLOTS, j, :], iota[:, :],
                                            relT[:, bass.ds(g, 1), j:j + 1].rearrange("p o k -> p (o k)"),
                                            wT[:, bass.ds(g, 1), j:j + 1].rearrange("p o k -> p (o k)"),
                                            ALU.is_equal, ALU.mult)
                ins.then_inc(S_ok, 1)

            for r in range(LEAD):
                weights_by_target(r, r, GPI)
            with dve.Fori(0, ROUNDS) as i:
                extra, lo, hi = round_numbers(dve, i, row)
                with dve.Fori(0, extra + 1) as w:
                    p = dve.snap(passes, min_val=0, max_val=1 << 20)
                    for r in range(GPI):
                        if r + LEAD < GPI:
                            weights_by_target(r + LEAD, i * GPI + (r + LEAD), p * GPI + (r + LEAD + 1 + GPI - SLOTS))
                        low_ = dve.snap(row[4 + r], min_val=0, max_val=NPAD - 1)
                        dve.reg_alu(base, low_ + w * WIN, NPAD, ALU.min)
                        to = dve.snap(base, min_val=0, max_val=NPAD)
                        dve.wait_ge(seg_mm, p * GPI + (r + GPI + 1))
                        dve.wait_ge(added, p * GPI + (r + WIN_BANKS))
                        window = aggv[:, :, bass.ds(to, WIN)]
                        dve.tensor_tensor(window, window,
                                          bank[r % WIN_BANKS][:, 0:KH * WIN].rearrange("p (h n) -> p h n", h=KH), ALU.add
                                          ).then_inc(added, 1)
                    dve.wait_ge(S_ok, p * GPI + GPI)
                    dve.sem_inc(hold, 1)
                    moved = relT[:, bass.ds(i * GPI, GPI), :]
                    dve.tensor_scalar(moved, moved, float(WIN), None, ALU.subtract).then_inc(shifted, 1)
                    dve.wait_ge(shifted, p + 2)
                    dve.reg_alu(following, w + 1, extra + 1, ALU.is_ge)
                    dve.reg_add(following, following, i)
                    dve.reg_alu(following, following, ROUNDS - 1, ALU.min)
                    nxt = dve.snap(following, min_val=0, max_val=ROUNDS - 1)
                    for r in range(LEAD):
                        weights_by_target(r, nxt * GPI + r, p * GPI + 2 * GPI)
                    dve.reg_add(passes, passes, 1)
                with dve.If(lo < hi):
                    with dve.Fori(lo, hi):
                        f = dve.snap(done, min_val=0, max_val=BATCHES - 1)
                        dve.wait_ge(added, dve.snap(passes, min_val=0, max_val=1 << 20) * GPI + WIN_BANKS)
                        dve.wait_ge(agg_tr, f + 1)
                        dve.sem_inc(hold, 1)
                        dve.tensor_scalar(aggS[:, :, :], aggv[:, :, bass.ds(f * BATCH, BATCH)], 0.0, None, ALU.max
                                          ).then_inc(relu_ok, 1)
                        place, before = dve.snap(side, min_val=0, max_val=2), dve.snap(other, min_val=0, max_val=2)
                        with dve.If(f > 0):
                            woven(route(dve.snap(mixed, min_val=0, max_val=BATCHES - 2)), tokens(f, place), 6)
                        with dve.If(f < 1):
                            alone(tokens(f, place))

                        def keep_tokens():
                            pair = xres[:, bass.ds(place, 2), :]
                            dve.wait_ge(tok_ok, f * 3 + 2)
                            dve.sem_inc(hold, 1)
                            dve.tensor_tensor(pair, pair, tokS[:, :, :], ALU.add).then_inc(tok_ok, 1)

                        def low_xT():
                            dve.wait_ge(xT_ok, f + 1)
                            dve.tensor_tensor(xT_low[:, :, :], bank[6][:, :].rearrange("p (h n) -> p h n", h=KH),
                                              xT[:, :, :].bitcast(FP32), ALU.subtract).then_inc(xT_low_ok, 1)
                        with dve.If(f > 0):
                            experts(dve.snap(mixed, min_val=0, max_val=BATCHES - 2), before, 2,
                                    ((EXP // 2, keep_tokens), (EXP - 2, low_xT)))
                            dve.reg_add(mixed, mixed, 1)
                        with dve.If(f < 1):
                            keep_tokens()
                            low_xT()
                        dve.reg_mov(kept, side)
                        dve.reg_mov(side, other)
                        dve.reg_mov(other, kept)
                        shift_logits(f)
                        dve.reg_add(done, done, 1)
            alone(route(BATCHES - 1))
            experts(BATCHES - 1, LAST_SIDE, LAST_TILES)

        @block.tensor
        def _(pe):
            pe.wait_ge(ident_ok, 1)
            pe.wait_ge(small_in, 48)
            for h in range(KH):
                ins = pe.transpose(bank[7][:, h * P:(h + 1) * P], small[:, h * P:(h + 1) * P], ident[:, :])
            ins.then_inc(small_tr, 1)
            pe.sem_inc(tr_done, 2)
            pe.sem_inc(mm_done, 16)

            def transposes(u, t):
                pe.wait_ge(ln_pair, t + 1)
                pe.wait_ge(hT_low_ok, t + 1)
                for h in range(KH):
                    ins = pe.transpose(bank[4 + u][:, h * P:(h + 1) * P], hn[:, u, h * P:(h + 1) * P], ident[:, :])
                ins.then_inc(tr_done, 1)

            def exact(dst_, pairs):
                for n, (left, right) in enumerate(pairs):
                    ins = pe.matmul(dst_, left, right, start=n == 0, stop=n == len(pairs) - 1)
                return ins

            def by_both_parts(dst_, high, low, weights, n):
                for h in range(KH):
                    pe.matmul(dst_, high[:, h, :], weights[:, h, :], start=h == 0, stop=False)
                    ins = pe.matmul(dst_[:, 0:n], low[:, h, :], weights[:, h, 0:n], start=False, stop=h == KH - 1)
                return ins

            def messages(u, t):
                pe.wait_ge(hT_low_ok, t + 3)
                pe.wait_ge(gate_ok, t + 1)
                high, low = hT[:, u, :, :], hT_low[:, u, :, :]
                by_both_parts(bank[6][:, 0:2 * R], high, low, gateT, R).then_inc(gate_mm, 1)
                for q in range(8):
                    pe.wait_ge(w_low_ok, q + 1)
                    pe.wait_ge((evac_act, evac_dve)[q % 2], t * 4 + (q // 2 + 1))
                    ins = exact(bank[q % 4][:, :], [pair for h in range(KH) for pair in (
                        (high[:, h, :], w_high[:, q, h, :]), (high[:, h, :], w_low[:, q, h, :]),
                        (low[:, h, :], w_high[:, q, h, :]))])
                    ins.then_inc(mm_done, 1)

            transposes(0, 0)
            pe.wait_ge(small_ok, 5)

            def part1(i0, i1):
                with pe.Fori(i0, i1) as i:
                    transposes(1, i * 2 + 1)
                    messages(0, i * 2)
                    transposes(0, i * 2 + 2)
                    messages(1, i * 2 + 1)

            part1(0, THIRD[1])
            pe.wait_ge(edges_ok, 1)
            pe.wait_ge(gate_ok, 2 * THIRD[1] + 1)
            for n, a in enumerate((0, 0, 1, 1, 3, 3)):
                if n >= 2:
                    pe.wait_ge(edge_ev[n % 2], n // 2)
                for j in range(4):
                    ins = pe.transpose(bank[7 if n % 2 == 0 else 6][:, j * P:(j + 1) * P],
                                       raw[:, a, n % 2, j * P:(j + 1) * P], ident[:, :])
                ins.then_inc(edge_tr, 1)
            pe.wait_ge(edge_ev[0], 3)
            pe.wait_ge(edge_ev[1], 3)
            part1(THIRD[1], TILES // 2)
            messages(0, TILES - 1)

            pe.wait_ge(evac_act, 4 * TILES + 2)
            pe.wait_ge(evac_dve, 4 * TILES + 2)
            pe.wait_ge(b2_in, 16)
            pe.wait_ge(tabs_ok, 1)
            pe.sem_inc(seg_mm, GPI)
            pe.sem_inc(agg_tr, 1)
            pe.sem_inc(y_mm, 2)
            pe.sem_inc(comb_tr, 1)
            passes = pe.alloc_register("passes")
            done = pe.alloc_register("batches")
            pe.reg_mov(passes, 0)
            pe.reg_mov(done, 0)
            row = [pe.alloc_register(f"row{k}") for k in range(4)]
            mixed = pe.alloc_register("mixed")
            pe.reg_mov(mixed, 0)

            def combine_T(b):
                pe.wait_ge(comb_ok, b + 1)
                for u in range(2):
                    ins = pe.transpose(bank[7][0:EXP, u * P:(u + 1) * P], comb[:, u, :], ident[:, :])
                ins.then_inc(comb_tr, 1)

            def hidden(b, e):
                pe.wait_ge(hid_ok, b * EXP + (e + 1))
                for m in range(KH):
                    ms = slice(m * P, (m + 1) * P)
                    ins = exact(bank[2 + e % 2][:, m * BATCH:(m + 1) * BATCH], [pair for h in range(KH) for pair in (
                        (w1_high[:, e, h, ms], xT[:, h, :]), (w1_high[:, e, h, ms], xT_low[:, h, :]),
                        (w1_low[:, e, h, ms], xT[:, h, :]))])
                ins.then_inc(h_mm, 1)

            def project(b, e, tiles=2):
                pe.wait_ge(hid_ok, b * EXP + (e + 3))
                if Y_BEFORE[e] is not None:
                    pe.wait_ge(y_added, b * (2 * EXP) + (tiles * (Y_BEFORE[e] + 1) + 2))
                for u in range(tiles):
                    for m in range(KH):
                        ins = pe.matmul(Y_BANK[e][:, u * F:(u + 1) * F], hid[:, e % 2, m, u * P:(u + 1) * P],
                                        w2s[:, e, m, :], start=m == 0, stop=m == KH - 1)
                ins.then_inc(y_mm, 1)

            def first_experts(b, tiles=2):
                pe.wait_ge(exp_in, KH * 16)
                pe.wait_ge(w1_low_ok, EXP + 1)
                p = pe.snap(passes, min_val=1, max_val=1 << 20)
                pe.wait_ge(added, p * GPI + (WIN_BANKS - 1))
                hidden(b, 0)
                pe.wait_ge(added, p * GPI + WIN_BANKS)
                hidden(b, 1)
                project(b, 0, tiles)
                hidden(b, 2)

            def experts(b, tiles=2, next_tokens=None):
                for e in range(1, EXP):
                    project(b, e, tiles)
                    if e + 2 < EXP:
                        hidden(b, e + 2)
                    if e == 2:
                        combine_T(b)
                    if e == BIAS_AT - 1:
                        pe.wait_ge(combT_ok, b + 1)
                        for u in range(2):
                            ins = pe.matmul(bank[7][:, u * F:(u + 1) * F], combT[:, u, :], b2s[:, :], start=True, stop=True)
                        ins.then_inc(bias_mm, 1)
                    if e == EXP - 3 and next_tokens is not None:
                        next_tokens()
                pe.wait_ge(y_added, b * (2 * EXP) + (tiles * 4 + 2))

            round_numbers(pe, 0, row)
            now = [pe.alloc_register(f"now{k}") for k in range(3)]
            with pe.Fori(0, ROUNDS) as i:
                for k in range(3):
                    pe.reg_mov(now[k], row[k])
                extra = pe.snap(now[0], min_val=0, max_val=NPAD // WIN)
                lo = pe.snap(now[1], min_val=0, max_val=BATCHES)
                hi = pe.snap(now[2], min_val=0, max_val=BATCHES)
                with pe.Fori(0, extra + 1):
                    p = pe.snap(passes, min_val=0, max_val=1 << 20)
                    for r in range(GPI):
                        if r == GPI // 2:
                            round_numbers(pe, i + 1, row)
                        pe.wait_ge(gathered[r], i * 64 + 64)
                        pe.wait_ge(S_ok, p * GPI + (r + 1))
                        pe.wait_ge(added, p * GPI + (r + 1))
                        for h in range(KH):
                            for j in range(4):
                                ins = pe.matmul(bank[r % WIN_BANKS][:, h * WIN:(h + 1) * WIN], ring[:, r * 4 + j, h * P:(h + 1) * P],
                                                S[:, r % SLOTS, j, :], start=j == 0, stop=j == 3)
                        ins.then_inc(seg_mm, 1)
                    pe.reg_add(passes, passes, 1)
                with pe.If(lo < hi):
                    with pe.Fori(lo, hi):
                        f = pe.snap(done, min_val=0, max_val=BATCHES - 1)
                        with pe.If(f > 0):
                            first_experts(pe.snap(mixed, min_val=0, max_val=BATCHES - 2))
                        pe.wait_ge(relu_ok, f + 1)
                        for u in range(2):
                            for h in range(KH):
                                ins = pe.transpose(bank[6][:, u * F + h * P:u * F + (h + 1) * P],
                                                   aggS[:, h, u * P:(u + 1) * P], ident[:, :])
                        ins.then_inc(agg_tr, 1)
                        def transpose_tokens():
                            pe.wait_ge(tok_ok, f * 3 + 2)
                            for h in range(KH):
                                for u in range(2):
                                    ins = pe.transpose(bank[6][:, h * BATCH + u * P:h * BATCH + (u + 1) * P],
                                                       tokS[:, u, h * P:(h + 1) * P], ident[:, :])
                            ins.then_inc(tok_tr, 1)
                        with pe.If(f > 0):
                            experts(pe.snap(mixed, min_val=0, max_val=BATCHES - 2), 2, transpose_tokens)
                            pe.reg_add(mixed, mixed, 1)
                        with pe.If(f < 1):
                            transpose_tokens()
                        pe.wait_ge(xT_low_ok, f + 1)
                        pe.wait_ge(bias_added, f + 1)
                        for u in range(2):
                            us = slice(u * P, (u + 1) * P)
                            ins = by_both_parts(bank[7][:, 2 * u * EXP:2 * (u + 1) * EXP], xT[:, :, us], xT_low[:, :, us],
                                                routerT, EXP)
                        ins.then_inc(logit_mm, 1)
                        pe.reg_add(done, done, 1)
            first_experts(BATCHES - 1, LAST_TILES)
            experts(BATCHES - 1, LAST_TILES)


_INPUTS = ["x", "src", "dst", "edge_type_16", "edge_weight1", "L0_gnn_weight", "L0_gnn_gate_weight",
           "L0_ffn_router_w", "L0_ffn_w1", "L0_ffn_b1", "L0_ffn_w2", "L0_ffn_b2"]


def kernel(**inputs):
    import numpy as np
    import concourse.bacc as bacc
    from concourse import mybir as mb
    from concourse.bass_utils import run_bass_kernel_spmd as run

    nc = bacc.Bacc("TRN2", target_bir_lowering=False, num_devices=1)
    arrays = {"in_" + k: np.ascontiguousarray(inputs[k]) for k in _INPUTS}
    args = [nc.dram_tensor(k, a.shape, mb.dt.from_np(a.dtype), kind="ExternalInput").ap() for k, a in arrays.items()]
    args.append(nc.dram_tensor("out", (N, F), mb.dt.float32, kind="ExternalOutput").ap())
    build(nc, *args)
    return run(nc, [arrays], core_ids=[0]).results[0]["out"]
```
